# Optimizing a Trainium2 kernel written in Bass

```python
import numpy as np
import jax
import jax.numpy as jnp

def _softmax(x, axis=-1):
    return jax.nn.softmax(x, axis=axis)

def _gelu(x):
    return jax.nn.gelu(x, approximate=True)

def _silu(x):
    return jax.nn.silu(x)

def _sigmoid(x):
    return jax.nn.sigmoid(x)

def _layernorm(x, axis=-1, eps=1e-05):
    m = jnp.mean(x, axis=axis, keepdims=True)
    v = jnp.var(x, axis=axis, keepdims=True)
    return (x - m) / jnp.sqrt(v + eps)

def _scatter_add(tgt, idx, src, axis=0):
    return tgt.at[idx].add(src)

def _segment_sum(src, seg, n):
    return jax.ops.segment_sum(src, seg, n)
kernel_name = 'mk_xattn_seq_d1_seqx_r2_a74199'

def setup_inputs(seed: int=0):
    np.random.seed(seed)
    _w = jnp.asarray

    def _rec_inputs():
        import jax
        import jax.numpy as jnp
        _rk = jax.random.key(seed)
        x = -0.000296 + 1 * jax.random.normal(jax.random.fold_in(_rk, 1), (2, 2048, 640), jnp.float32)
        _lenS = 2048 - jax.random.randint(jax.random.fold_in(_rk, 7), (2,), 0, max(1, 2048 // 4) + 1, jnp.int32)
        _lenS2 = 77 - jax.random.randint(jax.random.fold_in(_rk, 8), (2,), 0, max(1, 77 // 4) + 1, jnp.int32)
        _ctx_2048P = jax.random.normal(jax.random.fold_in(_rk, 11), (2, 16, 1024), jnp.float32)
        _ctx_2048c = jax.random.dirichlet(jax.random.fold_in(_rk, 511), 0.3 * jnp.ones((16,), jnp.float32), (2, 77))
        _ctx_2048t = jnp.einsum('bsk,bkd->bsd', _ctx_2048c, _ctx_2048P)
        _ctx_2048t = _ctx_2048t * jax.lax.rsqrt(jnp.mean(jnp.square(_ctx_2048t)) + 1e-12) * 0.953939
        ctx_2048 = 0.00118529 + 0.99962 * (_ctx_2048t + 0.3 * jax.random.normal(jax.random.fold_in(_rk, 611), (2, 77, 1024), jnp.float32))
        fside_Bx4x4_0 = jax.random.uniform(jax.random.fold_in(_rk, 12), (2, 4, 4), jnp.float32, 0.0, 0.981965)
        return (x, ctx_2048, fside_Bx4x4_0)
    x, ctx_2048, fside_Bx4x4_0 = _rec_inputs()

    def _L0_xattn_setup():
        import jax, jax.numpy as jnp
        import numpy as np
        HEADS = 20
        NUM_IP_TOKENS = 4
        NUM_DUMMY_TOKENS = 4
        IP_SCALE = 1.0
        ASPECT_RATIO = 1.0
        NEG = -10000.0

        def _grid_hw(seq_len, aspect_ratio):
            width = int((seq_len / aspect_ratio) ** 0.5)
            height = seq_len // width
            while width * height != seq_len:
                if width * height < seq_len:
                    width += 1
                else:
                    width -= 1
                height = seq_len // width
            return (height, width)

        def _sdpa(q, k, v, mask=None):
            dh = q.shape[-1]
            scores = jnp.einsum('bhqd,bhkd->bhqk', q, k) / jnp.sqrt(jnp.asarray(dh, q.dtype))
            if mask is not None:
                scores = scores + mask
            probs = jax.nn.softmax(scores, axis=-1)
            return jnp.einsum('bhqk,bhkd->bhqd', probs, v)

        def _split_heads(x, heads):
            b, l, d = x.shape
            return x.reshape(b, l, heads, d // heads).transpose(0, 2, 1, 3)

        def _merge_heads(x):
            b, h, l, dh = x.shape
            return x.transpose(0, 2, 1, 3).reshape(b, l, h * dh)

        def _ip_mask(bbox, batch_size, seq_len, dtype):
            M = bbox.shape[1]
            height, width = _grid_hw(seq_len, ASPECT_RATIO)
            x = jnp.linspace(0.0, 1.0, width, dtype=dtype)
            y = jnp.linspace(0.0, 1.0, height, dtype=dtype)
            yg, xg = jnp.meshgrid(y, x, indexing='ij')
            xg = xg.reshape(-1)
            yg = yg.reshape(-1)
            x1, y1, x2, y2 = (bbox[..., 0:1], bbox[..., 1:2], bbox[..., 2:3], bbox[..., 3:4])
            inside = (xg >= x1) & (xg <= x2) & (yg >= y1) & (yg <= y2)
            ip_mask = jnp.where(inside, 0.0, NEG).astype(dtype)
            ip_mask = jnp.transpose(ip_mask, (0, 2, 1))[:, None]
            ip_mask = jnp.repeat(ip_mask, NUM_IP_TOKENS // M, axis=-1)
            dummy = jnp.where(jnp.any(inside, axis=1), NEG, 0.0).astype(dtype)
            dummy = jnp.repeat(dummy[:, None, :, None], NUM_DUMMY_TOKENS, axis=-1)
            return jnp.concatenate([dummy, ip_mask], axis=-1)
        key = jax.random.key(seed)
        ks = jax.random.split(key, 12)
        B, S, D, C = (4, 2048, 640, 1024)
        text_len, M = (77, 4)
        hidden_states = jax.random.normal(ks[0], (B, S, D), jnp.float32)
        encoder_hidden_states = jax.random.normal(ks[1], (B, text_len + NUM_IP_TOKENS + NUM_DUMMY_TOKENS, C), jnp.float32)
        p1 = jax.random.uniform(ks[2], (B, M, 2), jnp.float32)
        p2 = jax.random.uniform(ks[3], (B, M, 2), jnp.float32)
        bbox = jnp.concatenate([jnp.minimum(p1, p2), jnp.maximum(p1, p2)], axis=-1)
        s = 0.02
        w_q = jax.random.normal(ks[4], (D, D), jnp.float32) * s
        w_k = jax.random.normal(ks[5], (C, D), jnp.float32) * s
        w_v = jax.random.normal(ks[6], (C, D), jnp.float32) * s
        w_k_ip = jax.random.normal(ks[7], (C, D), jnp.float32) * s
        w_v_ip = jax.random.normal(ks[8], (C, D), jnp.float32) * s
        w_out = jax.random.normal(ks[9], (D, D), jnp.float32) * s
        b_out = jnp.zeros((D,), jnp.float32)
        return {'hidden_states': hidden_states, 'encoder_hidden_states': encoder_hidden_states, 'bbox': bbox, 'w_q': w_q, 'w_k': w_k, 'w_v': w_v, 'w_k_ip': w_k_ip, 'w_v_ip': w_v_ip, 'w_out': w_out, 'b_out': b_out}
    _L0_xattn_all = _L0_xattn_setup()
    _L0_xattn_in = {k: v for k, v in _L0_xattn_all.items() if k in ('w_q', 'w_k', 'w_v', 'w_k_ip', 'w_v_ip', 'w_out', 'b_out')}
    del _L0_xattn_all
    return {'x': x, 'ctx_2048': ctx_2048, 'fside_Bx4x4_0': fside_Bx4x4_0, 'L0_xattn_w_q': _L0_xattn_in['w_q'], 'L0_xattn_w_k': _L0_xattn_in['w_k'], 'L0_xattn_w_v': _L0_xattn_in['w_v'], 'L0_xattn_w_k_ip': _L0_xattn_in['w_k_ip'], 'L0_xattn_w_v_ip': _L0_xattn_in['w_v_ip'], 'L0_xattn_w_out': _L0_xattn_in['w_out'], 'L0_xattn_b_out': _L0_xattn_in['b_out']}

def reference(x, ctx_2048, fside_Bx4x4_0, L0_xattn_w_q, L0_xattn_w_k, L0_xattn_w_v, L0_xattn_w_k_ip, L0_xattn_w_v_ip, L0_xattn_w_out, L0_xattn_b_out):
    import jax
    import jax.numpy as jnp

    def _L0_xattn_ref(hidden_states, encoder_hidden_states, bbox, w_q, w_k, w_v, w_k_ip, w_v_ip, w_out, b_out):
        import jax, jax.numpy as jnp
        import numpy as np
        HEADS = 20
        NUM_IP_TOKENS = 4
        NUM_DUMMY_TOKENS = 4
        IP_SCALE = 1.0
        ASPECT_RATIO = 1.0
        NEG = -10000.0

        def _grid_hw(seq_len, aspect_ratio):
            width = int((seq_len / aspect_ratio) ** 0.5)
            height = seq_len // width
            while width * height != seq_len:
                if width * height < seq_len:
                    width += 1
                else:
                    width -= 1
                height = seq_len // width
            return (height, width)

        def _sdpa(q, k, v, mask=None):
            dh = q.shape[-1]
            scores = jnp.einsum('bhqd,bhkd->bhqk', q, k) / jnp.sqrt(jnp.asarray(dh, q.dtype))
            if mask is not None:
                scores = scores + mask
            probs = jax.nn.softmax(scores, axis=-1)
            return jnp.einsum('bhqk,bhkd->bhqd', probs, v)

        def _split_heads(x, heads):
            b, l, d = x.shape
            return x.reshape(b, l, heads, d // heads).transpose(0, 2, 1, 3)

        def _merge_heads(x):
            b, h, l, dh = x.shape
            return x.transpose(0, 2, 1, 3).reshape(b, l, h * dh)

        def _ip_mask(bbox, batch_size, seq_len, dtype):
            M = bbox.shape[1]
            height, width = _grid_hw(seq_len, ASPECT_RATIO)
            x = jnp.linspace(0.0, 1.0, width, dtype=dtype)
            y = jnp.linspace(0.0, 1.0, height, dtype=dtype)
            yg, xg = jnp.meshgrid(y, x, indexing='ij')
            xg = xg.reshape(-1)
            yg = yg.reshape(-1)
            x1, y1, x2, y2 = (bbox[..., 0:1], bbox[..., 1:2], bbox[..., 2:3], bbox[..., 3:4])
            inside = (xg >= x1) & (xg <= x2) & (yg >= y1) & (yg <= y2)
            ip_mask = jnp.where(inside, 0.0, NEG).astype(dtype)
            ip_mask = jnp.transpose(ip_mask, (0, 2, 1))[:, None]
            ip_mask = jnp.repeat(ip_mask, NUM_IP_TOKENS // M, axis=-1)
            dummy = jnp.where(jnp.any(inside, axis=1), NEG, 0.0).astype(dtype)
            dummy = jnp.repeat(dummy[:, None, :, None], NUM_DUMMY_TOKENS, axis=-1)
            return jnp.concatenate([dummy, ip_mask], axis=-1)
        B, S, D = hidden_states.shape
        residual = hidden_states
        end_pos = encoder_hidden_states.shape[1] - (NUM_IP_TOKENS + NUM_DUMMY_TOKENS)
        text = encoder_hidden_states[:, :end_pos]
        ip_h = encoder_hidden_states[:, end_pos:]
        q = _split_heads(hidden_states @ w_q, HEADS)
        k = _split_heads(text @ w_k, HEADS)
        v = _split_heads(text @ w_v, HEADS)
        out_text = _sdpa(q, k, v)
        out_text = _merge_heads(out_text)
        mask_ip = _ip_mask(bbox, B, S, hidden_states.dtype)
        k_ip = _split_heads(ip_h @ w_k_ip, HEADS)
        v_ip = _split_heads(ip_h @ w_v_ip, HEADS)
        out_ip = _merge_heads(_sdpa(q, k_ip, v_ip, mask=mask_ip))
        out = out_text + IP_SCALE * out_ip
        out = out @ w_out + b_out
        out = out + residual
        return out
    x = _L0_xattn_ref(x, ctx_2048, fside_Bx4x4_0, L0_xattn_w_q, L0_xattn_w_k, L0_xattn_w_v, L0_xattn_w_k_ip, L0_xattn_w_v_ip, L0_xattn_w_out, L0_xattn_b_out)
    return x

_drawn_inputs = setup_inputs


def setup_inputs(seed=0):
    import zlib

    import numpy as np

    out = dict(_drawn_inputs(seed))
    spreads = {'L0_xattn_b_out': (0.0, 0.1)}
    factors = {'L0_xattn_w_k': 2.853}
    for name, (base, spread) in spreads.items():
        noise = np.random.default_rng([zlib.crc32(name.encode()), seed]).standard_normal(out[name].shape)
        drawn = base * np.exp(spread * noise) if base else spread * noise
        out[name] = jnp.asarray(drawn.astype(out[name].dtype))
    for name, factor in factors.items():
        out[name] = (out[name] * factor).astype(out[name].dtype)
    return out
```

```python
from contextlib import ExitStack

import concourse.bass as bass
from concourse import mybir

F32 = mybir.dt.float32
F32R = mybir.dt.float32r
ALU = mybir.AluOpType
ACT = mybir.ActivationFunctionType
AX_X = mybir.AxisListType.X

P = 128
BATCH, SEQ, D, C = 2, 2048, 640, 1024
HEADS, DH = 20, 32
DUMMY, IP = 4, 4
TOKENS = 77
TEXT = TOKENS - DUMMY - IP
IMG = DUMMY + IP
BOXES = 4
GRID_W, GRID_H = 64, 32
NEG = -10000.0
SCALE = float(DH) ** -0.5

KD = D // P
KC = C // P
HG = P // DH
GW = HG * TOKENS
W = 512
QT = W // P
TILES = SEQ // W
UNITS = BATCH * TILES * KD
PER_TURN = BATCH * KD
AHEAD_Q, AHEAD_S = 2, 1
BEHIND_OUT = KD


def xattn_kernel(nc, x, ctx, bbox, grid, eye, w_q, w_k, w_v, w_k_ip, w_v_ip, w_out, b_out, out):
    es = ExitStack()

    at = {}
    top = [-(-nc.sbuf_base // 32) * 32]

    def sb(name, shape, dt=F32):
        at[name] = top[0]
        n = 4
        for s in shape[1:]:
            n *= s
        top[0] += -(-n // 32) * 32
        assert top[0] <= nc.sbuf_usable_end, (name, top[0], nc.sbuf_usable_end)
        return nc.alloc_sbuf_tensor_at(name, shape, dt, offset=at[name])

    def over(name, owner, shape, offset=0):
        return nc.alloc_sbuf_tensor_at(name, shape, F32, offset=at[owner] + offset)

    def sem(name):
        return es.enter_context(nc.semaphore(name))

    with es:
        stage = sb("stage", [P, KD, D])
        x_hi = sb("x_hi", [P, BATCH, KD, W], F32R)
        x_lo = sb("x_lo", [P, BATCH, KD, W], F32R)
        wq_hi = sb("wq_hi", [P, KD, D], F32R)
        wq_lo = sb("wq_lo", [P, KD, D], F32R)
        wo_hi = sb("wo_hi", [P, KD, D], F32R)
        wo_lo = sb("wo_lo", [P, KD, D], F32R)
        k_hi = sb("k_hi", [P, BATCH, KD, GW], F32R)
        k_lo = sb("k_lo", [P, BATCH, KD, GW], F32R)
        v = sb("v", [P, BATCH, D])
        q_hi = sb("q_hi", [P, 2, W], F32R)
        q_lo = sb("q_lo", [P, 2, W], F32R)
        prob = sb("prob", [P, 2, QT, GW])
        prob_t = sb("prob_t", [P, HG, W])
        o_hi = sb("o_hi", [P, BATCH, KD, W], F32R)
        o_lo = sb("o_lo", [P, BATCH, KD, W], F32R)
        res = sb("res", [P, 2, W])
        ident = sb("ident", [P, P])
        mask = sb("mask", [P, BATCH, TILES, QT, IMG])
        bias = sb("bias", [P, KD])
        box = sb("box", [P, BATCH, BOXES, 4])
        grid_sb = sb("grid_sb", [P, 1 + TILES * QT])
        text_max = sb("text_max", [P, 2, QT, HG])
        img_max = sb("img_max", [P, 2, QT, HG])
        den = sb("den", [P, 2, 2, QT * HG])
        rden = sb("rden", [P, 2, 2, QT * HG])

        half, second = [P, KC // 2, D], KD * W * 4
        wk_raw = over("wk_raw0", "x_hi", half, second), over("wk_raw1", "x_lo", half, second)
        wki_raw = over("wki_raw0", "wo_hi", half), over("wki_raw1", "wo_lo", half)
        wv_raw = over("wv_raw0", "o_hi", half), over("wv_raw1", "o_lo", half)
        wvi_raw = over("wvi_raw0", "o_hi", half, second), over("wvi_raw1", "o_lo", half, second)

        spare = prob_t[:, :, :].rearrange("p a b -> p (a b)")
        ctx_sb = spare[:, 0:KC * BATCH * TOKENS].rearrange("p (k b n) -> p k b n", k=KC, b=BATCH)
        vt = spare[:, KC * BATCH * TOKENS:(KC + KD) * BATCH * TOKENS].rearrange("p (g b n) -> p g b n", g=KD, b=BATCH)

        ps = es.enter_context(nc.psum_tensor("ps", [P, 8, 512], F32))
        Q_BANK, OUT_BANK, T_BANK, O_BANK = 4, 5, 6, 7

        stage_loaded = [sem(f"stage_loaded{k}") for k in range(KD)]
        stage_hi = sem("stage_hi")
        stage_lo = sem("stage_lo")
        small_loaded = sem("small_loaded")
        ctx_loaded = sem("ctx_loaded")
        raw_loaded = {n: [sem(f"{n}_loaded{h}") for h in range(2)] for n in ("wk", "wki", "wv", "wvi")}
        zeroed = sem("zeroed")
        pad_zeroed = sem("pad_zeroed")
        mask_step = sem("mask_step")
        kt_made = sem("kt_made")
        k_hi_done = sem("k_hi_done")
        k_lo_done = sem("k_lo_done")
        vt_made = sem("vt_made")
        vt_copied = sem("vt_copied")
        v_made = sem("v_made")
        v_copied = sem("v_copied")
        q_made = sem("q_made")
        q_hi_done = sem("q_hi_done")
        q_lo_done = sem("q_lo_done")
        scores_made = sem("scores_made")
        scores_used = sem("scores_used")
        text_max_done = sem("text_max_done")
        img_max_done = sem("img_max_done")
        shifted = sem("shifted")
        exp_done = sem("exp_done")
        sums_done = sem("sums_done")
        rden_done = sem("rden_done")
        prob_done = sem("prob_done")
        t_made = sem("t_made")
        t_copied = sem("t_copied")
        o_made = sem("o_made")
        o_hi_done = sem("o_hi_done")
        o_lo_done = sem("o_lo_done")
        out_made = sem("out_made")
        res_loaded = [sem(f"res_loaded{k}") for k in range(2)]
        finished = sem("finished")
        stored = [sem(f"stored{k}") for k in range(2)]

        def num(i, c, each=1, plus=0):
            return i * (each * PER_TURN) + (each * c + plus)

        def place(i, c):
            return (c // KD) % BATCH, i + c // PER_TURN, c % KD

        def turns(eng, prologue, step, epilogue):
            prologue()
            for c in range(KD):
                step(0, c)
            with eng.Fori(0, (UNITS - PER_TURN) // PER_TURN) as i:
                for c in range(KD, KD + PER_TURN):
                    step(i, c)
            for c in range(UNITS - KD, UNITS):
                step(0, c)
            epilogue()

        def exists(i, c):
            return not isinstance(i, int) or 0 <= c < UNITS

        G_WQ, G_X0, G_X1, G_WO = range(4)

        def x_group(c):
            return c // KD + 2 if c // KD >= 2 else G_X0 + c // KD

        def stage_jobs(i, c):
            at = c % KD
            if at < 3:
                return [("x", c - at + KD + k) for k in (2 * at, 2 * at + 1) if k < KD and exists(i, c - at + KD)]
            if isinstance(i, int) and c < KD:
                return [("w_out", k) for k in ((0, 1, 2) if at == 3 else (3, 4))]
            return []

        block = es.enter_context(nc.Block())

        @block.sync
        def _(sp):
            def load(group, kt, dst_w, src, turn=0):
                job = group * KD + kt
                if group >= 1:
                    sp.wait_ge(stage_lo, turn + job - KD + 1)
                sp.dma_start(stage[:, kt, 0:dst_w], src).then_inc(stage_loaded[kt], 16)

            def residual(i, c):
                if not isinstance(i, int) or c >= 2:
                    sp.wait_ge(stored[c % 2], i * (16 * PER_TURN // 2) + 16 * (c // 2))
                sp.dma_start(res[:, c % 2, :], x[num(i, c)]).then_inc(res_loaded[c % 2], 16)

            def store(i, c):
                sp.wait_ge(finished, num(i, c, 1, 1))
                sp.dma_start(out[num(i, c)], res[:, c % 2, :]).then_inc(stored[c % 2], 16)

            def prologue():
                for kt in range(KD):
                    load(G_WQ, kt, D, w_q[kt])
                sp.dma_start(box[:, :, :, :], bbox).then_inc(small_loaded, 16)
                sp.dma_start(grid_sb[:, :], grid).then_inc(small_loaded, 16)
                sp.dma_start(bias[:, :], b_out).then_inc(small_loaded, 16)
                sp.dma_start(ident[:, :], eye).then_inc(small_loaded, 16)
                for kt in range(KD):
                    load(G_X0, kt, W, x[kt])

            def step(i, c):
                for what, k in stage_jobs(i, c):
                    if what == "x":
                        load(x_group(k), k % KD, W, x[num(i, k)], turn=i * PER_TURN)
                    else:
                        load(G_WO, k, D, w_out[k])
                if exists(i, c - BEHIND_OUT + 1):
                    residual(i, c - BEHIND_OUT + 1)
                if exists(i, c - BEHIND_OUT):
                    store(i, c - BEHIND_OUT)

            def epilogue():
                for c in range(UNITS - KD, UNITS):
                    if c + 1 < UNITS:
                        residual(0, c + 1)
                    store(0, c)
                for k in range(2):
                    sp.wait_ge(stored[k], 16 * (UNITS // 2))

            turns(sp, prologue, step, epilogue)

        @block.gpsimd
        def _(pool):
            def low(group, kt, turn, width, raw_chunk, hi, lo):
                job = group * KD + kt
                pool.wait_ge(stage_hi, turn + job + 1)
                nc.gpsimd.tensor_tensor(lo, raw_chunk, hi.bitcast(F32), ALU.subtract).then_inc(stage_lo, 1)

            def x_low(i, c):
                b, _, kt = place(i, c)
                low(x_group(c), kt, i * PER_TURN, W, stage[:, kt, 0:W], x_hi[:, b, kt, :], x_lo[:, b, kt, :])

            def prologue():
                nc.gpsimd.memset(k_hi[:, :, :, :].bitcast(F32), 0.0).then_inc(zeroed, 1)
                for kt in range(KD):
                    low(G_WQ, kt, 0, D, stage[:, kt, :], wq_hi[:, kt, :], wq_lo[:, kt, :])
                for kt in range(KD):
                    x_low(0, kt)

            def step(i, c):
                par = c % 2
                pool.wait_ge(rden_done, num(i, c, 1, 1))
                e = prob[:, par, :, :].rearrange("p q (h k) -> p (q h) k", k=TOKENS)
                nc.gpsimd.tensor_tensor(e[:, :, 0:TEXT], e[:, :, 0:TEXT],
                                        rden[:, par, 0, :].unsqueeze(2).to_broadcast([P, QT * HG, TEXT]), ALU.mult)
                nc.gpsimd.tensor_tensor(e[:, :, TEXT:TOKENS], e[:, :, TEXT:TOKENS],
                                        rden[:, par, 1, :].unsqueeze(2).to_broadcast([P, QT * HG, IMG]),
                                        ALU.mult).then_inc(prob_done, 1)
                for what, k in stage_jobs(i, c):
                    if what == "x":
                        x_low(i, k)
                    else:
                        low(G_WO, k, 0, D, stage[:, k, :], wo_hi[:, k, :], wo_lo[:, k, :])

            turns(pool, prologue, step, lambda: None)

        @block.scalar
        def _(act):
            def high(group, kt, turn, i16, raw_chunk, hi):
                act.wait_ge(stage_loaded[kt], i16 + 16 * (group + 1))
                nc.scalar.activation(hi, raw_chunk, ACT.Copy).then_inc(stage_hi, 1)

            def x_high(i, c):
                b, _, kt = place(i, c)
                if not isinstance(i, int) or c >= 2 * KD:
                    act.wait_ge(q_made, num(i, (c // KD - 1) * KD))
                high(x_group(c), kt, i * PER_TURN, i * (16 * BATCH), stage[:, kt, 0:W], x_hi[:, b, kt, :])

            def q_high(i, c):
                act.wait_ge(q_made, num(i, c, 1, 1))
                if not isinstance(i, int) or c >= 2:
                    act.wait_ge(scores_made, num(i, c - 2, 2, 2))
                nc.scalar.activation(q_hi[:, c % 2, :], ps[:, Q_BANK, :], ACT.Copy, scale=SCALE).then_inc(q_hi_done, 1)

            def exp(i, c):
                act.wait_ge(shifted, num(i, c, 1, 1))
                nc.scalar.activation(prob[:, c % 2, :, :], prob[:, c % 2, :, :], ACT.Exp).then_inc(exp_done, 1)

            def prologue():
                act.dma_start(ctx_sb, ctx).then_inc(ctx_loaded, 16)
                for name, pair, src in (("wk", wk_raw, w_k), ("wki", wki_raw, w_k_ip), ("wv", wv_raw, w_v), ("wvi", wvi_raw, w_v_ip)):
                    for h in range(2):
                        act.dma_start(pair[h][:, :, :],
                                      src[4 * h:4 * h + 4].rearrange("k p n -> p k n")).then_inc(raw_loaded[name][h], 16)
                for kt in range(KD):
                    high(G_WQ, kt, 0, 0, stage[:, kt, :], wq_hi[:, kt, :])
                for kt in range(KD):
                    x_high(0, kt)
                q_high(0, 0)
                act.wait_ge(zeroed, 2)
                for g in range(KD):
                    act.wait_ge(kt_made, g + 1)
                    for j in range(HG):
                        rows = slice(DH * j, DH * j + DH)
                        last = nc.scalar.activation(
                            k_hi[rows, :, g, TOKENS * j:TOKENS * j + TOKENS],
                            ps[rows, OUT_BANK + g % 3, 0:BATCH * TOKENS].rearrange("p (b n) -> p b n", b=BATCH), ACT.Copy)
                    last.then_inc(k_hi_done, 1)
                q_high(0, 1)
                for g in range(KD):
                    act.wait_ge(vt_made, g + 1)
                    nc.scalar.activation(vt[:, g, :, :],
                                         ps[:, OUT_BANK + g % 3, 0:BATCH * TOKENS].rearrange("p (b n) -> p b n", b=BATCH),
                                         ACT.Copy).then_inc(vt_copied, 1)
                act.wait_ge(v_made, 1)
                act.wait_ge(zeroed, 2)
                for b in range(BATCH):
                    nc.scalar.activation(v[0:TOKENS, b, 0:512], ps[0:TOKENS, OUT_BANK + b, :], ACT.Copy)
                nc.scalar.activation(v[0:TOKENS, :, 512:D],
                                     ps[0:TOKENS, OUT_BANK + 2, 0:BATCH * P].rearrange("p (b n) -> p b n", b=BATCH),
                                     ACT.Copy).then_inc(v_copied, 1)
                exp(0, 0)

            def step(i, c):
                b, t, g = place(i, c)
                for j in range(HG):
                    act.wait_ge(t_made, num(i, c, HG, j + 1))
                    if j == 0:
                        if isinstance(i, int) and c == 0:
                            act.wait_ge(pad_zeroed, 1)
                        else:
                            act.wait_ge(o_made, num(i, c))
                    nc.scalar.activation(prob_t[0:TOKENS, j, :], ps[0:TOKENS, T_BANK + j % 2, :], ACT.Copy).then_inc(t_copied, 1)
                    if j == 1 and exists(i, c + AHEAD_Q):
                        q_high(i, c + AHEAD_Q)
                    if j == 1 and exists(i, c + AHEAD_S):
                        exp(i, c + AHEAD_S)
                for what, k in stage_jobs(i, c):
                    if what == "x":
                        x_high(i, k)
                    else:
                        high(G_WO, k, 0, 0, stage[:, k, :], wo_hi[:, k, :])
                act.wait_ge(o_made, num(i, c, 1, 1))
                if not isinstance(i, int) or c >= 2 * KD:
                    act.wait_ge(out_made, num(i, (c // KD - 1) * KD))
                nc.scalar.activation(o_hi[:, b, g, :], ps[:, O_BANK, :], ACT.Copy).then_inc(o_hi_done, 1)

            turns(act, prologue, step, lambda: None)

        @block.vector
        def _(dve):
            def q_low(i, c):
                dve.wait_ge(q_hi_done, num(i, c, 1, 1))
                nc.vector.scalar_tensor_tensor(out=q_lo[:, c % 2, :], in0=ps[:, Q_BANK, :], scalar=SCALE,
                                               in1=q_hi[:, c % 2, :].bitcast(F32), op0=ALU.mult,
                                               op1=ALU.subtract).then_inc(q_lo_done, 1)

            def shift_pair(i, c, p):
                b, t, g = place(i, c)
                par, qs = c % 2, slice(2 * p, 2 * p + 2)
                s = ps[:, qs, 0:GW].rearrange("p q (h k) -> p q h k", k=TOKENS)
                e = prob[:, par, qs, :].rearrange("p q (h k) -> p q h k", k=TOKENS)
                dve.wait_ge(scores_made, num(i, c, 2, p + 1))
                nc.vector.tensor_reduce(text_max[:, par, qs, :], s[:, :, :, 0:TEXT], AX_X, ALU.max).then_inc(text_max_done, 1)
                if p == 0 and (not isinstance(i, int) or c >= 2):
                    dve.wait_ge(t_made, num(i, c - 2, HG, HG))
                nc.vector.tensor_tensor(e[:, :, :, TEXT:TOKENS], s[:, :, :, TEXT:TOKENS],
                                        mask[:, b, t, qs, :].unsqueeze(2).to_broadcast([P, 2, HG, IMG]), ALU.add)
                dve.wait_ge(text_max_done, num(i, c, 2, p + 1))
                nc.vector.tensor_tensor(e[:, :, :, 0:TEXT], s[:, :, :, 0:TEXT],
                                        text_max[:, par, qs, :].unsqueeze(3).to_broadcast([P, 2, HG, TEXT]),
                                        ALU.subtract).then_inc(scores_used, 1)

            def shift_img(i, c):
                par = c % 2
                e = prob[:, par, :, :].rearrange("p q (h k) -> p (q h) k", k=TOKENS)[:, :, TEXT:TOKENS]
                m = img_max[:, par, :, :].rearrange("p q h -> p (q h)")
                dve.wait_ge(scores_used, num(i, c, 2, 2))
                nc.vector.tensor_reduce(m, e, AX_X, ALU.max).then_inc(img_max_done, 1)
                dve.wait_ge(img_max_done, num(i, c, 1, 1))
                nc.vector.tensor_tensor(e, e, m.unsqueeze(2).to_broadcast([P, QT * HG, IMG]),
                                        ALU.subtract).then_inc(shifted, 1)

            def sums(i, c):
                par = c % 2
                e = prob[:, par, :, :].rearrange("p q (h k) -> p (q h) k", k=TOKENS)
                dve.wait_ge(exp_done, num(i, c, 1, 1))
                nc.vector.tensor_reduce(den[:, par, 0, :], e[:, :, 0:TEXT], AX_X, ALU.add)
                nc.vector.tensor_reduce(den[:, par, 1, :], e[:, :, TEXT:TOKENS], AX_X, ALU.add).then_inc(sums_done, 1)
                dve.wait_ge(sums_done, num(i, c, 1, 1))
                if not isinstance(i, int) or c >= 2:
                    dve.wait_ge(prob_done, num(i, c - 2, 1, 1))
                nc.vector.reciprocal(rden[:, par, :, :], den[:, par, :, :]).then_inc(rden_done, 1)

            def finish(i, c):
                dve.wait_ge(out_made, num(i, c, 1, 1))
                dve.wait_ge(res_loaded[c % 2], i * (16 * PER_TURN // 2) + 16 * (c // 2 + 1))
                nc.vector.scalar_tensor_tensor(out=res[:, c % 2, :], in0=ps[:, OUT_BANK, :],
                                               scalar=bias[:, c % KD:c % KD + 1], in1=res[:, c % 2, :],
                                               op0=ALU.add, op1=ALU.add).then_inc(finished, 1)

            def masks():
                steps = [0]

                def then(ins):
                    steps[0] += 1
                    ins.then_inc(mask_step, 1)
                    dve.wait_ge(mask_step, steps[0])

                blocks = [P, TILES * QT, BOXES]
                gx = grid_sb[:, 0:1].unsqueeze(2).to_broadcast(blocks)
                gy = grid_sb[:, 1:].unsqueeze(2).to_broadcast(blocks)
                inside = prob[:, 0, 0, 0:BATCH * TILES * QT * BOXES].rearrange("p (b t m) -> p b t m", b=BATCH, m=BOXES)
                test = prob[:, 0, 1, 0:BATCH * TILES * QT * BOXES].rearrange("p (b t m) -> p b t m", b=BATCH, m=BOXES)
                any_in = prob[:, 0, 2, 0:BATCH * TILES * QT].rearrange("p (b t) -> p b t", b=BATCH)
                dve.wait_ge(small_loaded, 64)
                for b in range(BATCH):
                    edge = [box[:, b, :, k].unsqueeze(1).to_broadcast(blocks) for k in range(4)]
                    then(nc.vector.tensor_tensor(inside[:, b], gx, edge[0], ALU.is_ge))
                    for coord, side, op in ((gx, 2, ALU.is_le), (gy, 1, ALU.is_ge), (gy, 3, ALU.is_le)):
                        then(nc.vector.tensor_tensor(test[:, b], coord, edge[side], op))
                        then(nc.vector.tensor_tensor(inside[:, b], inside[:, b], test[:, b], ALU.mult))
                    m = mask[:, b, :, :, :].rearrange("p t q k -> p (t q) k")
                    then(nc.vector.tensor_scalar(m[:, :, DUMMY:IMG], inside[:, b], -NEG, NEG, ALU.mult, ALU.add))
                    then(nc.vector.tensor_reduce(any_in[:, b], inside[:, b], AX_X, ALU.max))
                    then(nc.vector.tensor_scalar(m[:, :, 0:DUMMY],
                                                 any_in[:, b].unsqueeze(2).to_broadcast([P, TILES * QT, DUMMY]),
                                                 NEG, None, ALU.mult))

            def prologue():
                nc.vector.memset(v[:, :, :], 0.0)
                nc.vector.memset(k_lo[:, :, :, :].bitcast(F32), 0.0).then_inc(zeroed, 1)
                masks()
                q_low(0, 0)
                dve.wait_ge(zeroed, 2)
                for g in range(KD):
                    dve.wait_ge(k_hi_done, g + 1)
                    for j in range(HG):
                        rows = slice(DH * j, DH * j + DH)
                        cols = slice(TOKENS * j, TOKENS * j + TOKENS)
                        last = nc.vector.tensor_tensor(
                            k_lo[rows, :, g, cols],
                            ps[rows, OUT_BANK + g % 3, 0:BATCH * TOKENS].rearrange("p (b n) -> p b n", b=BATCH),
                            k_hi[rows, :, g, cols].bitcast(F32), ALU.subtract)
                    last.then_inc(k_lo_done, 1)
                for p in range(2):
                    shift_pair(0, 0, p)
                shift_img(0, 0)
                q_low(0, 1)
                sums(0, 0)
                dve.wait_ge(v_made, 1)
                nc.vector.memset(prob_t[64:P, :, :], 0.0).then_inc(pad_zeroed, 1)

            def step(i, c):
                if exists(i, c + AHEAD_S):
                    shift_pair(i, c + AHEAD_S, 0)
                if exists(i, c - 1):
                    o_low(i, c - 1)
                if exists(i, c + AHEAD_S):
                    shift_pair(i, c + AHEAD_S, 1)
                    shift_img(i, c + AHEAD_S)
                if exists(i, c - BEHIND_OUT):
                    finish(i, c - BEHIND_OUT)
                if exists(i, c + AHEAD_Q):
                    q_low(i, c + AHEAD_Q)
                if exists(i, c + AHEAD_S):
                    sums(i, c + AHEAD_S)

            def o_low(i, c):
                b, t, g = place(i, c)
                dve.wait_ge(o_hi_done, num(i, c, 1, 1))
                nc.vector.tensor_tensor(o_lo[:, b, g, :], ps[:, O_BANK, :], o_hi[:, b, g, :].bitcast(F32),
                                        ALU.subtract).then_inc(o_lo_done, 1)

            def epilogue():
                o_low(0, UNITS - 1)
                for c in range(UNITS - KD, UNITS):
                    finish(0, c)

            turns(dve, prologue, step, epilogue)

        @block.tensor
        def _(pe):
            def three_pass(bank, w_hi, w_lo, m_hi, m_lo, b, g, part):
                cols = slice(P * g, P * g + P)
                steps = [s for kt in range(KD) for s in ((w_hi, m_hi, kt), (w_hi, m_lo, kt), (w_lo, m_hi, kt))]
                for n in part:
                    w, m, kt = steps[n]
                    last = nc.tensor.matmul(ps[:, bank, :], w[:, kt, cols], m[:, b, kt, :],
                                            start=(n == 0), stop=(n == len(steps) - 1))
                return last

            def make_q(i, c, part):
                b, t, g = place(i, c)
                if part[0] == 0:
                    if not isinstance(i, int) or c >= 1:
                        pe.wait_ge(q_lo_done, num(i, c))
                    if g == 0:
                        pe.wait_ge(stage_lo, (i * PER_TURN) + (x_group(c) + 1) * KD)
                last = three_pass(Q_BANK, wq_hi, wq_lo, x_hi, x_lo, b, g, part)
                if part[-1] == 3 * KD - 1:
                    last.then_inc(q_made, 1)

            def make_scores(i, c, p):
                b, t, g = place(i, c)
                if p == 0:
                    pe.wait_ge(q_lo_done, num(i, c, 1, 1))
                if not isinstance(i, int) or c >= 1:
                    pe.wait_ge(scores_used, num(i, c - 1, 2, p + 1))
                for q in (2 * p, 2 * p + 1):
                    blk = slice(P * q, P * q + P)
                    o = ps[:, q, 0:GW]
                    nc.tensor.matmul(o, q_hi[:, c % 2, blk], k_hi[:, b, g, :], start=True, stop=False)
                    nc.tensor.matmul(o, q_hi[:, c % 2, blk], k_lo[:, b, g, :], start=False, stop=False)
                    last = nc.tensor.matmul(o, q_lo[:, c % 2, blk], k_hi[:, b, g, :], start=False, stop=True)
                last.then_inc(scores_made, 1)

            def transpose(i, c, j):
                if j == 0:
                    pe.wait_ge(prob_done, num(i, c, 1, 1))
                    if not isinstance(i, int) or c >= 1:
                        pe.wait_ge(t_copied, num(i, c - 1, HG, HG - 1))
                elif j == 1:
                    if not isinstance(i, int) or c >= 1:
                        pe.wait_ge(o_lo_done, num(i, c))
                else:
                    pe.wait_ge(t_copied, num(i, c, HG, j - 1))
                for q in range(QT):
                    last = nc.tensor.transpose(ps[0:TOKENS, T_BANK + j % 2, P * q:P * q + P],
                                               prob[:, c % 2, q, TOKENS * j:TOKENS * j + TOKENS], ident[:, :])
                last.then_inc(t_made, 1)

            def make_o(i, c):
                b, t, g = place(i, c)
                pe.wait_ge(t_copied, num(i, c, HG, HG))
                for j in range(HG):
                    last = nc.tensor.matmul(ps[DH * j:DH * j + DH, O_BANK, :],
                                            v[:, b, P * g + DH * j:P * g + DH * j + DH], prob_t[:, j, :],
                                            start=True, stop=True)
                last.then_inc(o_made, 1)

            def make_out(i, c, part):
                b, t, g = place(i, c)
                if part[0] == 0:
                    if g == 0:
                        pe.wait_ge(o_lo_done, num(i, c, 1, KD))
                        if c // KD % BATCH == 0:
                            pe.wait_ge(stage_lo, (G_WO + 1) * KD)
                    if not isinstance(i, int) or c >= 1:
                        pe.wait_ge(finished, num(i, c))
                last = three_pass(OUT_BANK, wo_hi, wo_lo, o_hi, o_lo, b, g, part)
                if part[-1] == 3 * KD - 1:
                    last.then_inc(out_made, 1)

            def project_ctx(name, raw_text, name_ip, raw_ip, made, freed):
                for g in range(KD):
                    if g >= 3:
                        pe.wait_ge(freed, g - 2)
                    bank = ps[:, OUT_BANK + g % 3, 0:BATCH * TOKENS].rearrange("p (b n) -> p b n", b=BATCH)
                    for which, r, cols in ((name, raw_text, slice(0, TEXT)), (name_ip, raw_ip, slice(TEXT, TOKENS))):
                        for kt in range(KC):
                            if g == 0 and kt % 4 == 0:
                                pe.wait_ge(raw_loaded[which][kt // 4], 16)
                            last = nc.tensor.matmul(bank[:, :, cols], r[kt // 4][:, kt % 4, P * g:P * g + P],
                                                    ctx_sb[:, kt, :, cols], start=(kt == 0), stop=(kt == KC - 1))
                    last.then_inc(made, 1)

            whole = range(3 * KD)

            def prologue():
                make_q(0, 0, whole)
                pe.wait_ge(ctx_loaded, 16)
                project_ctx("wk", wk_raw, "wki", wki_raw, kt_made, k_lo_done)
                make_q(0, 1, whole)
                pe.wait_ge(k_lo_done, KD)
                for p in range(2):
                    make_scores(0, 0, p)
                project_ctx("wv", wv_raw, "wvi", wvi_raw, vt_made, vt_copied)
                pe.wait_ge(vt_copied, KD)
                pe.wait_ge(small_loaded, 64)
                for b in range(BATCH):
                    for g in range(KD):
                        bank, col = (OUT_BANK + b, P * g) if g < 4 else (OUT_BANK + 2, P * b)
                        last = nc.tensor.transpose(ps[0:TOKENS, bank, col:col + P], vt[:, g, b, :], ident[:, :])
                last.then_inc(v_made, 1)
                pe.wait_ge(v_copied, 1)

            def step(i, c):
                ahead, behind = exists(i, c + AHEAD_S), exists(i, c - BEHIND_OUT)
                if ahead:
                    make_scores(i, c + AHEAD_S, 0)
                if behind:
                    make_out(i, c - BEHIND_OUT, whole[0:8])
                if ahead:
                    make_scores(i, c + AHEAD_S, 1)
                if behind:
                    make_out(i, c - BEHIND_OUT, whole[8:15])
                for j in range(HG):
                    transpose(i, c, j)
                    if exists(i, c + AHEAD_Q):
                        make_q(i, c + AHEAD_Q, whole[4 * j:min(4 * j + 4, 15)])
                make_o(i, c)

            def epilogue():
                for c in range(UNITS - KD, UNITS):
                    make_out(0, c, whole)

            turns(pe, prologue, step, epilogue)


def kernel(x, ctx_2048, fside_Bx4x4_0, L0_xattn_w_q, L0_xattn_w_k, L0_xattn_w_v, L0_xattn_w_k_ip,
           L0_xattn_w_v_ip, L0_xattn_w_out, L0_xattn_b_out):
    import numpy as np
    import concourse.bacc as bacc
    from concourse.bass_utils import run_bass_kernel_spmd

    xs = np.arange(GRID_W, dtype=np.float32) / np.float32(GRID_W - 1)
    ys = np.arange(GRID_H, dtype=np.float32) / np.float32(GRID_H - 1)
    p = np.arange(P)
    blocks = np.arange(TILES * QT)
    grid = np.concatenate([xs[p % GRID_W][:, None], ys[2 * blocks[None, :] + p[:, None] // GRID_W]], axis=1)

    def chunks(w):
        return np.asarray(w).reshape(-1, P, D)

    arrays = {
        "x": np.asarray(x).reshape(BATCH, TILES, W, KD, P).transpose(1, 0, 3, 4, 2).reshape(UNITS, P, W),
        "ctx": np.asarray(ctx_2048).reshape(BATCH, TOKENS, KC, P).transpose(3, 2, 0, 1),
        "bbox": np.broadcast_to(np.asarray(fside_Bx4x4_0)[None], (P, BATCH, BOXES, 4)),
        "grid": grid,
        "eye": np.eye(P, dtype=np.float32),
        "w_q": chunks(L0_xattn_w_q), "w_k": chunks(L0_xattn_w_k), "w_v": chunks(L0_xattn_w_v),
        "w_k_ip": chunks(L0_xattn_w_k_ip), "w_v_ip": chunks(L0_xattn_w_v_ip), "w_out": chunks(L0_xattn_w_out),
        "b_out": np.asarray(L0_xattn_b_out).reshape(KD, P).T,
    }
    arrays = {k: np.ascontiguousarray(a) for k, a in arrays.items()}
    nc = bacc.Bacc("TRN2", target_bir_lowering=False, num_devices=1)
    args = {k: nc.dram_tensor(f"in_{k}", a.shape, F32, kind="ExternalInput").ap() for k, a in arrays.items()}
    out = nc.dram_tensor("out_tiles", (UNITS, P, W), F32, kind="ExternalOutput").ap()
    xattn_kernel(nc, **args, out=out)
    r = run_bass_kernel_spmd(nc, [{f"in_{k}": a for k, a in arrays.items()}], core_ids=[0])
    got = np.asarray(r.results[0]["out_tiles"])
    return np.ascontiguousarray(got.reshape(TILES, BATCH, KD, P, W).transpose(1, 0, 4, 2, 3).reshape(BATCH, SEQ, D))
```

```python
from contextlib import ExitStack

import concourse.bass as bass
from concourse import mybir

F32 = mybir.dt.float32
F32R = mybir.dt.float32r
ALU = mybir.AluOpType
ACT = mybir.ActivationFunctionType
AX_X = mybir.AxisListType.X

P = 128
BATCH, SEQ, D, C = 2, 2048, 640, 1024
HEADS, DH = 20, 32
DUMMY, IP = 4, 4
TOKENS = 77
TEXT = TOKENS - DUMMY - IP
IMG = DUMMY + IP
IMG_PAD = 32
CTX_COLS = 2 * TEXT + IMG_PAD
BOXES = 4
GRID_W, GRID_H = 64, 32
NEG = -10000.0
SCALE = float(DH) ** -0.5

KD = D // P
KC = C // P
HG = P // DH
GW = HG * TOKENS
W = 512
QT = W // P
TILES = SEQ // W
UNITS = BATCH * TILES * KD
PER_TURN = BATCH * KD
AHEAD_Q, AHEAD_S = 2, 1
BEHIND_OUT = KD


def xattn_kernel(nc, x, ctx, bbox, grid, eye, w_q, w_k, w_v, w_k_ip, w_v_ip, w_out, b_out, out):
    es = ExitStack()

    at = {}
    top = [-(-nc.sbuf_base // 32) * 32]

    def sb(name, shape, dt=F32):
        at[name] = top[0]
        n = 4
        for s in shape[1:]:
            n *= s
        top[0] += -(-n // 32) * 32
        assert top[0] <= nc.sbuf_usable_end, (name, top[0], nc.sbuf_usable_end)
        return nc.alloc_sbuf_tensor_at(name, shape, dt, offset=at[name])

    def over(name, owner, shape, offset=0):
        return nc.alloc_sbuf_tensor_at(name, shape, F32, offset=at[owner] + offset)

    def sem(name):
        return es.enter_context(nc.semaphore(name))

    with es:
        stage = sb("stage", [P, KD, D])
        x_hi = sb("x_hi", [P, BATCH, KD, W], F32R)
        x_lo = sb("x_lo", [P, BATCH, KD, W], F32R)
        wq_hi = sb("wq_hi", [P, KD, D], F32R)
        wq_lo = sb("wq_lo", [P, KD, D], F32R)
        wo_hi = sb("wo_hi", [P, KD, D], F32R)
        wo_lo = sb("wo_lo", [P, KD, D], F32R)
        k_hi = sb("k_hi", [P, BATCH, KD, GW], F32R)
        k_lo = sb("k_lo", [P, BATCH, KD, GW], F32R)
        v = sb("v", [P, BATCH, D])
        q_hi = sb("q_hi", [P, 2, W], F32R)
        q_lo = sb("q_lo", [P, 2, W], F32R)
        prob = sb("prob", [P, 2, QT, GW])
        prob_t = sb("prob_t", [P, HG, W])
        o_hi = sb("o_hi", [P, BATCH, KD, W], F32R)
        o_lo = sb("o_lo", [P, BATCH, KD, W], F32R)
        res = sb("res", [P, 2, W])
        eye_sb = sb("eye_sb", [P, P + BATCH * IMG])
        ident = eye_sb[:, 0:P]
        fold = eye_sb[:, P:P + BATCH * IMG]
        mask = sb("mask", [P, BATCH, TILES, QT, IMG])
        bias = sb("bias", [P, KD])
        box = sb("box", [P, BATCH, BOXES, 4])
        grid_sb = sb("grid_sb", [P, 1 + TILES * QT])
        text_max = sb("text_max", [P, 2, QT, HG])
        img_max = sb("img_max", [P, 2, QT, HG])
        den = sb("den", [P, 2, 2, QT * HG])
        rden = sb("rden", [P, 2, 2, QT * HG])

        half, second = [P, KC // 2, D], KD * W * 4
        wk_raw = over("wk_raw0", "x_hi", half, second), over("wk_raw1", "x_lo", half, second)
        wki_raw = over("wki_raw0", "wo_hi", half), over("wki_raw1", "wo_lo", half)
        wv_raw = over("wv_raw0", "o_hi", half), over("wv_raw1", "o_lo", half)
        wvi_raw = over("wvi_raw0", "o_hi", half, second), over("wvi_raw1", "o_lo", half, second)

        ctx_sb = over("ctx_sb", "prob_t", [P, KC, CTX_COLS])
        img_part = over("img_part", "prob_t", [P, D], KC * CTX_COLS * 4)
        vt = over("vt", "prob", [P, KD, BATCH, TOKENS], QT * GW * 4)
        assert KC * CTX_COLS + D <= HG * W and KD * BATCH * TOKENS <= QT * GW

        ps = es.enter_context(nc.psum_tensor("ps", [P, 8, 512], F32))
        Q_BANK, OUT_BANK, T_BANK, O_BANK = 4, 5, 6, 7
        LAST_BANKS = Q_BANK, OUT_BANK

        stage_loaded = [sem(f"stage_loaded{k}") for k in range(KD)]
        stage_hi = sem("stage_hi")
        stage_lo = sem("stage_lo")
        small_loaded = sem("small_loaded")
        ctx_loaded = sem("ctx_loaded")
        raw_loaded = {n: [sem(f"{n}_loaded{h}") for h in range(2)] for n in ("wk", "wki", "wv", "wvi")}
        zeroed = sem("zeroed")
        part_made = sem("part_made")
        part_copied = sem("part_copied")
        pad_zeroed = sem("pad_zeroed")
        mask_step = sem("mask_step")
        kt_made = sem("kt_made")
        k_hi_done = sem("k_hi_done")
        k_lo_done = sem("k_lo_done")
        vt_made = sem("vt_made")
        vt_copied = sem("vt_copied")
        v_made = sem("v_made")
        v_copied = sem("v_copied")
        q_made = sem("q_made")
        q_hi_done = sem("q_hi_done")
        q_lo_done = sem("q_lo_done")
        scores_made = sem("scores_made")
        scores_used = sem("scores_used")
        text_max_done = sem("text_max_done")
        img_max_done = sem("img_max_done")
        shifted = sem("shifted")
        exp_done = sem("exp_done")
        sums_done = sem("sums_done")
        rden_done = sem("rden_done")
        prob_done = sem("prob_done")
        t_made = sem("t_made")
        t_copied = sem("t_copied")
        o_made = sem("o_made")
        o_hi_done = sem("o_hi_done")
        o_lo_done = sem("o_lo_done")
        out_made = sem("out_made")
        res_loaded = [sem(f"res_loaded{k}") for k in range(2)]
        finished = sem("finished")
        stored = [sem(f"stored{k}") for k in range(2)]

        def num(i, c, each=1, plus=0):
            return i * (each * PER_TURN) + (each * c + plus)

        def place(i, c):
            return (c // KD) % BATCH, i + c // PER_TURN, c % KD

        def turns(eng, prologue, step, epilogue):
            prologue()
            for c in range(KD):
                step(0, c)
            with eng.Fori(0, (UNITS - PER_TURN) // PER_TURN) as i:
                for c in range(KD, KD + PER_TURN):
                    step(i, c)
            for c in range(UNITS - KD, UNITS):
                step(0, c)
            epilogue()

        def exists(i, c):
            return not isinstance(i, int) or 0 <= c < UNITS

        G_WQ, G_X0, G_X1, G_WO = range(4)

        def x_group(c):
            return c // KD + 2 if c // KD >= 2 else G_X0 + c // KD

        def stage_jobs(i, c):
            at = c % KD
            if at < 3:
                return [("x", c - at + KD + k) for k in (2 * at, 2 * at + 1) if k < KD and exists(i, c - at + KD)]
            if isinstance(i, int) and c < KD:
                return [("w_out", k) for k in ((0, 1, 2) if at == 3 else (3, 4))]
            return []

        def load_raw(eng, name, pair, src):
            for h in range(2):
                eng.dma_start(pair[h][:, :, :],
                              src[4 * h:4 * h + 4].rearrange("k p n -> p k n")).then_inc(raw_loaded[name][h], 16)

        block = es.enter_context(nc.Block())

        @block.sync
        def _(sp):
            def load(group, kt, dst_w, src, turn=0):
                job = group * KD + kt
                if group >= 1:
                    sp.wait_ge(stage_lo, turn + job - KD + 1)
                sp.dma_start(stage[:, kt, 0:dst_w], src).then_inc(stage_loaded[kt], 16)

            def residual(i, c):
                if not isinstance(i, int) or c >= 2:
                    sp.wait_ge(stored[c % 2], i * (16 * PER_TURN // 2) + 16 * (c // 2))
                sp.dma_start(res[:, c % 2, :], x[num(i, c)]).then_inc(res_loaded[c % 2], 16)

            def store(i, c):
                sp.wait_ge(finished, num(i, c, 1, 1))
                sp.dma_start(out[num(i, c)], res[:, c % 2, :]).then_inc(stored[c % 2], 16)

            def prologue():
                for kt in range(KD):
                    load(G_WQ, kt, D, w_q[kt])
                sp.dma_start(box[:, :, :, :], bbox).then_inc(small_loaded, 16)
                sp.dma_start(grid_sb[:, :], grid).then_inc(small_loaded, 16)
                sp.dma_start(bias[:, :], b_out).then_inc(small_loaded, 16)
                sp.dma_start(eye_sb[:, :], eye).then_inc(small_loaded, 16)
                for kt in range(KD):
                    load(G_X0, kt, W, x[kt])
                load_raw(sp, "wvi", wvi_raw, w_v_ip)
                load_raw(sp, "wv", wv_raw, w_v)

            def step(i, c):
                for what, k in stage_jobs(i, c):
                    if what == "x":
                        load(x_group(k), k % KD, W, x[num(i, k)], turn=i * PER_TURN)
                    else:
                        load(G_WO, k, D, w_out[k])
                if exists(i, c - BEHIND_OUT + 1):
                    residual(i, c - BEHIND_OUT + 1)
                if exists(i, c - BEHIND_OUT):
                    store(i, c - BEHIND_OUT)

            def epilogue():
                for c in range(UNITS - KD, UNITS):
                    if c + 1 < UNITS:
                        residual(0, c + 1)
                    store(0, c)
                for k in range(2):
                    sp.wait_ge(stored[k], 16 * (UNITS // 2))

            turns(sp, prologue, step, epilogue)

        @block.gpsimd
        def _(pool):
            def low(group, kt, turn, width, raw_chunk, hi, lo):
                job = group * KD + kt
                pool.wait_ge(stage_hi, turn + job + 1)
                nc.gpsimd.tensor_tensor(lo, raw_chunk, hi.bitcast(F32), ALU.subtract).then_inc(stage_lo, 1)

            def x_low(i, c):
                b, _, kt = place(i, c)
                low(x_group(c), kt, i * PER_TURN, W, stage[:, kt, 0:W], x_hi[:, b, kt, :], x_lo[:, b, kt, :])

            def prologue():
                for kt in range(KD):
                    low(G_WQ, kt, 0, D, stage[:, kt, :], wq_hi[:, kt, :], wq_lo[:, kt, :])
                for kt in range(KD):
                    x_low(0, kt)

            def step(i, c):
                par = c % 2
                pool.wait_ge(rden_done, num(i, c, 1, 1))
                e = prob[:, par, :, :].rearrange("p q (h k) -> p (q h) k", k=TOKENS)
                nc.gpsimd.tensor_tensor(e[:, :, 0:TEXT], e[:, :, 0:TEXT],
                                        rden[:, par, 0, :].unsqueeze(2).to_broadcast([P, QT * HG, TEXT]), ALU.mult)
                nc.gpsimd.tensor_tensor(e[:, :, TEXT:TOKENS], e[:, :, TEXT:TOKENS],
                                        rden[:, par, 1, :].unsqueeze(2).to_broadcast([P, QT * HG, IMG]),
                                        ALU.mult).then_inc(prob_done, 1)
                for what, k in stage_jobs(i, c):
                    if what == "x":
                        x_low(i, k)
                    else:
                        low(G_WO, k, 0, D, stage[:, k, :], wo_hi[:, k, :], wo_lo[:, k, :])

            turns(pool, prologue, step, lambda: None)

        @block.scalar
        def _(act):
            def high(group, kt, turn, i16, raw_chunk, hi):
                act.wait_ge(stage_loaded[kt], i16 + 16 * (group + 1))
                nc.scalar.activation(hi, raw_chunk, ACT.Copy).then_inc(stage_hi, 1)

            def x_high(i, c):
                b, _, kt = place(i, c)
                if not isinstance(i, int) or c >= 2 * KD:
                    act.wait_ge(q_made, num(i, (c // KD - 1) * KD))
                high(x_group(c), kt, i * PER_TURN, i * (16 * BATCH), stage[:, kt, 0:W], x_hi[:, b, kt, :])

            def q_high(i, c):
                act.wait_ge(q_made, num(i, c, 1, 1))
                if not isinstance(i, int) or c >= 2:
                    act.wait_ge(scores_made, num(i, c - 2, 2, 2))
                nc.scalar.activation(q_hi[:, c % 2, :], ps[:, Q_BANK, :], ACT.Copy, scale=SCALE).then_inc(q_hi_done, 1)

            def exp(i, c):
                act.wait_ge(shifted, num(i, c, 1, 1))
                nc.scalar.activation(prob[:, c % 2, :, :], prob[:, c % 2, :, :], ACT.Exp).then_inc(exp_done, 1)

            def prologue():
                act.dma_start(ctx_sb[:, :, :], ctx).then_inc(ctx_loaded, 16)
                load_raw(act, "wki", wki_raw, w_k_ip)
                load_raw(act, "wk", wk_raw, w_k)
                for kt in range(KD):
                    high(G_WQ, kt, 0, 0, stage[:, kt, :], wq_hi[:, kt, :])
                copy_part(0)
                for kt in range(KD):
                    x_high(0, kt)
                act.wait_ge(zeroed, 1)
                for g in range(KD):
                    act.wait_ge(kt_made, g + 1)
                    for j in range(HG):
                        rows = slice(DH * j, DH * j + DH)
                        last = nc.scalar.activation(
                            k_hi[rows, :, g, TOKENS * j:TOKENS * j + TOKENS],
                            ps[rows, OUT_BANK + g % 3, 0:BATCH * TOKENS].rearrange("p (b n) -> p b n", b=BATCH), ACT.Copy)
                    last.then_inc(k_hi_done, 1)
                q_high(0, 0)
                q_high(0, 1)
                copy_part(1)
                exp(0, 0)
                for g in range(KD):
                    act.wait_ge(vt_made, g + 1)
                    nc.scalar.activation(vt[:, g, :, :],
                                         ps[:, OUT_BANK + g % 3, 0:BATCH * TOKENS].rearrange("p (b n) -> p b n", b=BATCH),
                                         ACT.Copy).then_inc(vt_copied, 1)
                act.wait_ge(v_made, 1)
                for b in range(BATCH):
                    nc.scalar.activation(v[0:TOKENS, b, 0:512], ps[0:TOKENS, OUT_BANK + b, :], ACT.Copy)
                nc.scalar.activation(v[0:TOKENS, :, 512:D],
                                     ps[0:TOKENS, OUT_BANK + 2, 0:BATCH * P].rearrange("p (b n) -> p b n", b=BATCH),
                                     ACT.Copy).then_inc(v_copied, 1)

            def copy_part(n):
                act.wait_ge(part_made, n + 1)
                nc.scalar.activation(img_part[:, 0:512], ps[:, T_BANK, :], ACT.Copy)
                nc.scalar.activation(img_part[:, 512:D], ps[:, O_BANK, 0:D - 512], ACT.Copy).then_inc(part_copied, 1)

            def step(i, c):
                b, t, g = place(i, c)
                if exists(i, c + AHEAD_Q):
                    q_high(i, c + AHEAD_Q)
                for j in range(HG):
                    act.wait_ge(t_made, num(i, c, HG, j + 1))
                    if j == 0:
                        if isinstance(i, int) and c == 0:
                            act.wait_ge(pad_zeroed, 1)
                        else:
                            act.wait_ge(o_made, num(i, c))
                    nc.scalar.activation(prob_t[0:TOKENS, j, :], ps[0:TOKENS, T_BANK + j % 2, :], ACT.Copy).then_inc(t_copied, 1)
                    if j == 0 and exists(i, c + AHEAD_S):
                        exp(i, c + AHEAD_S)
                for what, k in stage_jobs(i, c):
                    if what == "x":
                        x_high(i, k)
                    else:
                        high(G_WO, k, 0, 0, stage[:, k, :], wo_hi[:, k, :])
                act.wait_ge(o_made, num(i, c, 1, 1))
                if not isinstance(i, int) or c >= 2 * KD:
                    act.wait_ge(out_made, num(i, (c // KD - 1) * KD))
                nc.scalar.activation(o_hi[:, b, g, :], ps[:, O_BANK, :], ACT.Copy).then_inc(o_hi_done, 1)

            turns(act, prologue, step, lambda: None)

        @block.vector
        def _(dve):
            def q_low(i, c):
                dve.wait_ge(q_hi_done, num(i, c, 1, 1))
                nc.vector.scalar_tensor_tensor(out=q_lo[:, c % 2, :], in0=ps[:, Q_BANK, :], scalar=SCALE,
                                               in1=q_hi[:, c % 2, :].bitcast(F32), op0=ALU.mult,
                                               op1=ALU.subtract).then_inc(q_lo_done, 1)

            def shift_pair(i, c, p):
                b, t, g = place(i, c)
                par, qs = c % 2, slice(2 * p, 2 * p + 2)
                s = ps[:, qs, 0:GW].rearrange("p q (h k) -> p q h k", k=TOKENS)
                e = prob[:, par, qs, :].rearrange("p q (h k) -> p q h k", k=TOKENS)
                dve.wait_ge(scores_made, num(i, c, 2, p + 1))
                nc.vector.tensor_reduce(text_max[:, par, qs, :], s[:, :, :, 0:TEXT], AX_X, ALU.max).then_inc(text_max_done, 1)
                if p == 0 and (not isinstance(i, int) or c >= 2):
                    dve.wait_ge(t_made, num(i, c - 2, HG, HG))
                nc.vector.tensor_tensor(e[:, :, :, TEXT:TOKENS], s[:, :, :, TEXT:TOKENS],
                                        mask[:, b, t, qs, :].unsqueeze(2).to_broadcast([P, 2, HG, IMG]), ALU.add)
                dve.wait_ge(text_max_done, num(i, c, 2, p + 1))
                nc.vector.tensor_tensor(e[:, :, :, 0:TEXT], s[:, :, :, 0:TEXT],
                                        text_max[:, par, qs, :].unsqueeze(3).to_broadcast([P, 2, HG, TEXT]),
                                        ALU.subtract).then_inc(scores_used, 1)

            def shift_img(i, c):
                par = c % 2
                e = prob[:, par, :, :].rearrange("p q (h k) -> p (q h) k", k=TOKENS)[:, :, TEXT:TOKENS]
                m = img_max[:, par, :, :].rearrange("p q h -> p (q h)")
                dve.wait_ge(scores_used, num(i, c, 2, 2))
                nc.vector.tensor_reduce(m, e, AX_X, ALU.max).then_inc(img_max_done, 1)
                dve.wait_ge(img_max_done, num(i, c, 1, 1))
                nc.vector.tensor_tensor(e, e, m.unsqueeze(2).to_broadcast([P, QT * HG, IMG]),
                                        ALU.subtract).then_inc(shifted, 1)

            def sums(i, c):
                par = c % 2
                e = prob[:, par, :, :].rearrange("p q (h k) -> p (q h) k", k=TOKENS)
                dve.wait_ge(exp_done, num(i, c, 1, 1))
                nc.vector.tensor_reduce(den[:, par, 0, :], e[:, :, 0:TEXT], AX_X, ALU.add)
                nc.vector.tensor_reduce(den[:, par, 1, :], e[:, :, TEXT:TOKENS], AX_X, ALU.add).then_inc(sums_done, 1)
                dve.wait_ge(sums_done, num(i, c, 1, 1))
                if not isinstance(i, int) or c >= 2:
                    dve.wait_ge(prob_done, num(i, c - 2, 1, 1))
                nc.vector.reciprocal(rden[:, par, :, :], den[:, par, :, :]).then_inc(rden_done, 1)

            def finish(i, c, bank=OUT_BANK):
                dve.wait_ge(out_made, num(i, c, 1, 1))
                dve.wait_ge(res_loaded[c % 2], i * (16 * PER_TURN // 2) + 16 * (c // 2 + 1))
                nc.vector.scalar_tensor_tensor(out=res[:, c % 2, :], in0=ps[:, bank, :],
                                               scalar=bias[:, c % KD:c % KD + 1], in1=res[:, c % 2, :],
                                               op0=ALU.add, op1=ALU.add).then_inc(finished, 1)

            def masks():
                steps = [0]

                def then(ins):
                    steps[0] += 1
                    ins.then_inc(mask_step, 1)
                    dve.wait_ge(mask_step, steps[0])

                blocks = [P, TILES * QT, BOXES]
                gx = grid_sb[:, 0:1].unsqueeze(2).to_broadcast(blocks)
                gy = grid_sb[:, 1:].unsqueeze(2).to_broadcast(blocks)
                inside = prob[:, 0, 0, 0:BATCH * TILES * QT * BOXES].rearrange("p (b t m) -> p b t m", b=BATCH, m=BOXES)
                test = prob[:, 0, 1, 0:BATCH * TILES * QT * BOXES].rearrange("p (b t m) -> p b t m", b=BATCH, m=BOXES)
                any_in = prob[:, 0, 2, 0:BATCH * TILES * QT].rearrange("p (b t) -> p b t", b=BATCH)
                dve.wait_ge(small_loaded, 64)
                for b in range(BATCH):
                    edge = [box[:, b, :, k].unsqueeze(1).to_broadcast(blocks) for k in range(4)]
                    then(nc.vector.tensor_tensor(inside[:, b], gx, edge[0], ALU.is_ge))
                    for coord, side, op in ((gx, 2, ALU.is_le), (gy, 1, ALU.is_ge), (gy, 3, ALU.is_le)):
                        then(nc.vector.tensor_tensor(test[:, b], coord, edge[side], op))
                        then(nc.vector.tensor_tensor(inside[:, b], inside[:, b], test[:, b], ALU.mult))
                    m = mask[:, b, :, :, :].rearrange("p t q k -> p (t q) k")
                    then(nc.vector.tensor_scalar(m[:, :, DUMMY:IMG], inside[:, b], -NEG, NEG, ALU.mult, ALU.add))
                    then(nc.vector.tensor_reduce(any_in[:, b], inside[:, b], AX_X, ALU.max))
                    then(nc.vector.tensor_scalar(m[:, :, 0:DUMMY],
                                                 any_in[:, b].unsqueeze(2).to_broadcast([P, TILES * QT, DUMMY]),
                                                 NEG, None, ALU.mult))

            def prologue():
                nc.vector.memset(k_hi[:, :, :, :].bitcast(F32), 0.0)
                nc.vector.memset(k_lo[:, :, :, :].bitcast(F32), 0.0)
                nc.vector.memset(v[:, :, :], 0.0).then_inc(zeroed, 1)
                masks()
                dve.wait_ge(zeroed, 1)
                for g in range(KD):
                    dve.wait_ge(k_hi_done, g + 1)
                    for j in range(HG):
                        rows = slice(DH * j, DH * j + DH)
                        cols = slice(TOKENS * j, TOKENS * j + TOKENS)
                        last = nc.vector.tensor_tensor(
                            k_lo[rows, :, g, cols],
                            ps[rows, OUT_BANK + g % 3, 0:BATCH * TOKENS].rearrange("p (b n) -> p b n", b=BATCH),
                            k_hi[rows, :, g, cols].bitcast(F32), ALU.subtract)
                    last.then_inc(k_lo_done, 1)
                q_low(0, 0)
                shift_pair(0, 0, 0)
                q_low(0, 1)
                shift_pair(0, 0, 1)
                shift_img(0, 0)
                sums(0, 0)
                dve.wait_ge(v_made, 1)
                nc.vector.memset(prob_t[64:P, :, :], 0.0).then_inc(pad_zeroed, 1)

            def step(i, c):
                if exists(i, c + AHEAD_S):
                    shift_pair(i, c + AHEAD_S, 0)
                if exists(i, c - 1):
                    o_low(i, c - 1)
                if exists(i, c + AHEAD_S):
                    shift_pair(i, c + AHEAD_S, 1)
                    shift_img(i, c + AHEAD_S)
                if exists(i, c + AHEAD_Q):
                    q_low(i, c + AHEAD_Q)
                if exists(i, c + AHEAD_S):
                    sums(i, c + AHEAD_S)
                if exists(i, c - BEHIND_OUT):
                    finish(i, c - BEHIND_OUT)

            def o_low(i, c):
                b, t, g = place(i, c)
                dve.wait_ge(o_hi_done, num(i, c, 1, 1))
                nc.vector.tensor_tensor(o_lo[:, b, g, :], ps[:, O_BANK, :], o_hi[:, b, g, :].bitcast(F32),
                                        ALU.subtract).then_inc(o_lo_done, 1)

            def epilogue():
                o_low(0, UNITS - 1)
                for c in range(UNITS - KD, UNITS):
                    finish(0, c, LAST_BANKS[c % 2])

            turns(dve, prologue, step, epilogue)

        @block.tensor
        def _(pe):
            def three_pass(bank, w_hi, w_lo, m_hi, m_lo, b, g, part):
                cols = slice(P * g, P * g + P)
                steps = [s for kt in range(KD) for s in ((w_hi, m_hi, kt), (w_hi, m_lo, kt), (w_lo, m_hi, kt))]
                for n in part:
                    w, m, kt = steps[n]
                    last = nc.tensor.matmul(ps[:, bank, :], w[:, kt, cols], m[:, b, kt, :],
                                            start=(n == 0), stop=(n == len(steps) - 1))
                return last

            def make_q(i, c, part):
                b, t, g = place(i, c)
                if part[0] == 0:
                    if not isinstance(i, int) or c >= 1:
                        pe.wait_ge(q_lo_done, num(i, c))
                    if g == 0:
                        pe.wait_ge(stage_lo, (i * PER_TURN) + (x_group(c) + 1) * KD)
                last = three_pass(Q_BANK, wq_hi, wq_lo, x_hi, x_lo, b, g, part)
                if part[-1] == 3 * KD - 1:
                    last.then_inc(q_made, 1)

            def make_scores(i, c, p):
                b, t, g = place(i, c)
                if p == 0:
                    pe.wait_ge(q_lo_done, num(i, c, 1, 1))
                    if isinstance(i, int) and c == 0:
                        pe.wait_ge(k_lo_done, KD)
                if not isinstance(i, int) or c >= 1:
                    pe.wait_ge(scores_used, num(i, c - 1, 2, p + 1))
                for q in (2 * p, 2 * p + 1):
                    blk = slice(P * q, P * q + P)
                    o = ps[:, q, 0:GW]
                    nc.tensor.matmul(o, q_hi[:, c % 2, blk], k_hi[:, b, g, :], start=True, stop=False)
                    nc.tensor.matmul(o, q_hi[:, c % 2, blk], k_lo[:, b, g, :], start=False, stop=False)
                    last = nc.tensor.matmul(o, q_lo[:, c % 2, blk], k_hi[:, b, g, :], start=False, stop=True)
                last.then_inc(scores_made, 1)

            def transpose(i, c, j):
                if j == 0:
                    pe.wait_ge(prob_done, num(i, c, 1, 1))
                    if not isinstance(i, int) or c >= 1:
                        pe.wait_ge(t_copied, num(i, c - 1, HG, HG - 1))
                elif j == 1:
                    if not isinstance(i, int) or c >= 1:
                        pe.wait_ge(o_lo_done, num(i, c))
                else:
                    pe.wait_ge(t_copied, num(i, c, HG, j - 1))
                for q in range(QT):
                    last = nc.tensor.transpose(ps[0:TOKENS, T_BANK + j % 2, P * q:P * q + P],
                                               prob[:, c % 2, q, TOKENS * j:TOKENS * j + TOKENS], ident)
                last.then_inc(t_made, 1)

            def make_o(i, c):
                b, t, g = place(i, c)
                pe.wait_ge(t_copied, num(i, c, HG, HG))
                for j in range(HG):
                    last = nc.tensor.matmul(ps[DH * j:DH * j + DH, O_BANK, :],
                                            v[:, b, P * g + DH * j:P * g + DH * j + DH], prob_t[:, j, :],
                                            start=True, stop=True)
                last.then_inc(o_made, 1)

            def make_out(i, c, part, bank=OUT_BANK, free=0):
                b, t, g = place(i, c)
                if part[0] == 0:
                    if g == 0:
                        pe.wait_ge(o_lo_done, num(i, c, 1, KD))
                        if c // KD % BATCH == 0:
                            pe.wait_ge(stage_lo, (G_WO + 1) * KD)
                    if not isinstance(i, int) or c >= 1:
                        pe.wait_ge(finished, num(i, c, 1, -free))
                last = three_pass(bank, wo_hi, wo_lo, o_hi, o_lo, b, g, part)
                if part[-1] == 3 * KD - 1:
                    last.then_inc(out_made, 1)

            def image_part(n, name, raw):
                for kt in range(KC):
                    if kt % 4 == 0:
                        pe.wait_ge(raw_loaded[name][kt // 4], 16)
                        if n == 1 and kt == 0:
                            pe.wait_ge(k_lo_done, KD)
                    rows = slice(IMG_PAD * (kt % 4), IMG_PAD * (kt % 4) + IMG_PAD)
                    for bank, cols in ((T_BANK, slice(0, 512)), (O_BANK, slice(512, D))):
                        last = nc.tensor.matmul(ps[rows, bank, 0:cols.stop - cols.start],
                                                ctx_sb[:, kt, BATCH * TEXT:CTX_COLS], raw[kt // 4][:, kt % 4, cols],
                                                start=(kt < 4), stop=(kt >= 4))
                last.then_inc(part_made, 1)

            def project_ctx(n, name, raw, made, freed):
                for g in range(KD):
                    if g >= 3:
                        pe.wait_ge(freed, g - 2)
                    bank = ps[:, OUT_BANK + g % 3, 0:BATCH * TOKENS].rearrange("p (b n) -> p b n", b=BATCH)
                    for kt in range(KC):
                        if g == 0 and kt % 4 == 0:
                            pe.wait_ge(raw_loaded[name][kt // 4], 16)
                        text = ctx_sb[:, kt, 0:BATCH * TEXT].rearrange("p (b n) -> p b n", b=BATCH)
                        nc.tensor.matmul(bank[:, :, 0:TEXT], raw[kt // 4][:, kt % 4, P * g:P * g + P], text,
                                         start=(kt == 0), stop=(kt == KC - 1))
                    if g == 0:
                        pe.wait_ge(part_copied, n + 1)
                        pe.wait_ge(small_loaded, 64)
                    nc.tensor.matmul(bank[:, :, TEXT:TOKENS], img_part[:, P * g:P * g + P],
                                     fold.rearrange("p (b n) -> p b n", b=BATCH),
                                     start=True, stop=True).then_inc(made, 1)

            whole = range(3 * KD)

            def prologue():
                pe.wait_ge(ctx_loaded, 16)
                image_part(0, "wki", wki_raw)
                project_ctx(0, "wk", wk_raw, kt_made, k_lo_done)
                make_q(0, 0, whole)
                make_scores(0, 0, 0)
                make_q(0, 1, whole)
                make_scores(0, 0, 1)
                image_part(1, "wvi", wvi_raw)
                project_ctx(1, "wv", wv_raw, vt_made, vt_copied)
                pe.wait_ge(vt_copied, KD)
                for b in range(BATCH):
                    for g in range(KD):
                        bank, col = (OUT_BANK + b, P * g) if g < 4 else (OUT_BANK + 2, P * b)
                        last = nc.tensor.transpose(ps[0:TOKENS, bank, col:col + P], vt[:, g, b, :], ident)
                last.then_inc(v_made, 1)

            def step(i, c):
                if exists(i, c + AHEAD_S):
                    make_scores(i, c + AHEAD_S, 0)
                if exists(i, c + AHEAD_Q):
                    make_q(i, c + AHEAD_Q, whole[0:8])
                if exists(i, c + AHEAD_S):
                    make_scores(i, c + AHEAD_S, 1)
                if exists(i, c + AHEAD_Q):
                    make_q(i, c + AHEAD_Q, whole[8:15])
                if isinstance(i, int) and c == 0:
                    pe.wait_ge(v_copied, 1)
                for j in range(HG):
                    transpose(i, c, j)
                    if exists(i, c - BEHIND_OUT):
                        make_out(i, c - BEHIND_OUT, whole[4 * j:min(4 * j + 4, 15)])
                make_o(i, c)

            def epilogue():
                for c in range(UNITS - KD, UNITS):
                    make_out(0, c, whole, LAST_BANKS[c % 2], free=(c > UNITS - KD))

            turns(pe, prologue, step, epilogue)


def kernel(x, ctx_2048, fside_Bx4x4_0, L0_xattn_w_q, L0_xattn_w_k, L0_xattn_w_v, L0_xattn_w_k_ip,
           L0_xattn_w_v_ip, L0_xattn_w_out, L0_xattn_b_out):
    import numpy as np
    import concourse.bacc as bacc
    from concourse.bass_utils import run_bass_kernel_spmd

    xs = np.arange(GRID_W, dtype=np.float32) / np.float32(GRID_W - 1)
    ys = np.arange(GRID_H, dtype=np.float32) / np.float32(GRID_H - 1)
    p = np.arange(P)
    blocks = np.arange(TILES * QT)
    grid = np.concatenate([xs[p % GRID_W][:, None], ys[2 * blocks[None, :] + p[:, None] // GRID_W]], axis=1)

    def chunks(w):
        return np.asarray(w).reshape(-1, P, D)

    tokens = np.asarray(ctx_2048).reshape(BATCH, TOKENS, KC, P).transpose(3, 2, 0, 1)
    text = tokens[:, :, :, 0:TEXT].reshape(P, KC, BATCH * TEXT)
    image = tokens[:, :, :, TEXT:].reshape(P, KC, BATCH * IMG)
    arrays = {
        "x": np.asarray(x).reshape(BATCH, TILES, W, KD, P).transpose(1, 0, 3, 4, 2).reshape(UNITS, P, W),
        "ctx": np.concatenate([text, image, np.zeros((P, KC, IMG_PAD - BATCH * IMG), np.float32)], axis=2),
        "bbox": np.broadcast_to(np.asarray(fside_Bx4x4_0)[None], (P, BATCH, BOXES, 4)),
        "grid": grid,
        "eye": np.concatenate([np.eye(P), (p % IMG_PAD)[:, None] == np.arange(BATCH * IMG)], axis=1).astype(np.float32),
        "w_q": chunks(L0_xattn_w_q), "w_k": chunks(L0_xattn_w_k), "w_v": chunks(L0_xattn_w_v),
        "w_k_ip": chunks(L0_xattn_w_k_ip), "w_v_ip": chunks(L0_xattn_w_v_ip), "w_out": chunks(L0_xattn_w_out),
        "b_out": np.asarray(L0_xattn_b_out).reshape(KD, P).T,
    }
    arrays = {k: np.ascontiguousarray(a) for k, a in arrays.items()}
    nc = bacc.Bacc("TRN2", target_bir_lowering=False, num_devices=1)
    args = {k: nc.dram_tensor(f"in_{k}", a.shape, F32, kind="ExternalInput").ap() for k, a in arrays.items()}
    out = nc.dram_tensor("out_tiles", (UNITS, P, W), F32, kind="ExternalOutput").ap()
    xattn_kernel(nc, **args, out=out)
    r = run_bass_kernel_spmd(nc, [{f"in_{k}": a for k, a in arrays.items()}], core_ids=[0])
    got = np.asarray(r.results[0]["out_tiles"])
    return np.ascontiguousarray(got.reshape(TILES, BATCH, KD, P, W).transpose(1, 0, 4, 2, 3).reshape(BATCH, SEQ, D))
```

```python
from contextlib import ExitStack

import concourse.bass as bass
from concourse import mybir

F32 = mybir.dt.float32
F32R = mybir.dt.float32r
ALU = mybir.AluOpType
ACT = mybir.ActivationFunctionType
AX_X = mybir.AxisListType.X

P = 128
BATCH, SEQ, D, C = 2, 2048, 640, 1024
HEADS, DH = 20, 32
DUMMY, IP = 4, 4
TOKENS = 77
TEXT = TOKENS - DUMMY - IP
IMG = DUMMY + IP
IMG_PAD = 32
CTX_COLS = 2 * TEXT + IMG_PAD
BOXES = 4
GRID_W, GRID_H = 64, 32
NEG = -10000.0
SCALE = float(DH) ** -0.5

KD = D // P
KC = C // P
HG = P // DH
GW = HG * TOKENS
W = 512
QT = W // P
TILES = SEQ // W
UNITS = BATCH * TILES * KD
PER_TURN = BATCH * KD
AHEAD_Q, AHEAD_S = 2, 1
LATE = KD - 2
BEHIND_OUT = KD


def xattn_kernel(nc, x, ctx, bbox, grid, eye, w_q, w_k, w_v, w_k_ip, w_v_ip, w_out, b_out, out):
    es = ExitStack()

    at = {}
    top = [-(-nc.sbuf_base // 32) * 32]

    def sb(name, shape, dt=F32):
        at[name] = top[0]
        n = 4
        for s in shape[1:]:
            n *= s
        top[0] += -(-n // 32) * 32
        assert top[0] <= nc.sbuf_usable_end, (name, top[0], nc.sbuf_usable_end)
        return nc.alloc_sbuf_tensor_at(name, shape, dt, offset=at[name])

    def over(name, owner, shape, offset=0):
        return nc.alloc_sbuf_tensor_at(name, shape, F32, offset=at[owner] + offset)

    def sem(name):
        return es.enter_context(nc.semaphore(name))

    with es:
        stage = sb("stage", [P, KD, D])
        x_hi = sb("x_hi", [P, BATCH, KD, W], F32R)
        x_lo = sb("x_lo", [P, BATCH, KD, W], F32R)
        wq_hi = sb("wq_hi", [P, KD, D], F32R)
        wq_lo = sb("wq_lo", [P, KD, D], F32R)
        wo_hi = sb("wo_hi", [P, KD, D], F32R)
        wo_lo = sb("wo_lo", [P, KD, D], F32R)
        k_hi = sb("k_hi", [P, BATCH, KD, GW], F32R)
        k_lo = sb("k_lo", [P, BATCH, KD, GW], F32R)
        v = sb("v", [P, BATCH, D])
        q_hi = sb("q_hi", [P, 2, W], F32R)
        q_lo = sb("q_lo", [P, 2, W], F32R)
        prob = sb("prob", [P, 2, QT, GW])
        prob_t = sb("prob_t", [P, HG, W])
        o_hi = sb("o_hi", [P, BATCH, KD, W], F32R)
        o_lo = sb("o_lo", [P, BATCH, KD, W], F32R)
        eye_sb = sb("eye_sb", [P, P + BATCH * IMG])
        ident = eye_sb[:, 0:P]
        fold = eye_sb[:, P:P + BATCH * IMG]
        mask = sb("mask", [P, BATCH, TILES, QT, IMG])
        bias = sb("bias", [P, KD])
        box = sb("box", [P, BATCH, BOXES, 4])
        grid_sb = sb("grid_sb", [P, 1 + TILES * QT])
        text_max = sb("text_max", [P, 2, QT, HG])
        img_max = sb("img_max", [P, 2, QT, HG])
        den = sb("den", [P, 2, 2, QT * HG])
        rden = sb("rden", [P, 2, 2, QT * HG])
        res = sb("res", [P, 2, W])

        half, second = [P, KC // 2, D], KD * W * 4
        wk_raw = over("wk_raw0", "x_hi", half, second), over("wk_raw1", "x_lo", half, second)
        wki_raw = over("wki_raw0", "wo_hi", half), over("wki_raw1", "wo_lo", half)
        wv_raw = over("wv_raw0", "o_hi", half, second), over("wv_raw1", "o_lo", half, second)
        wvi_raw = over("wvi_raw0", "o_hi", half), over("wvi_raw1", "o_lo", half)

        ctx_sb = over("ctx_sb", "res", [P, KC, CTX_COLS])
        img_part = over("img_part", "res", [P, D], KC * CTX_COLS * 4)
        assert at["res"] + (KC * CTX_COLS + D) * 4 <= nc.sbuf_usable_end
        vt = over("vt", "o_hi", [P, BATCH, TOKENS], (KD - 1) * W * 4)

        ps = es.enter_context(nc.psum_tensor("ps", [P, 8, 512], F32))
        Q_BANK, OUT_BANK, T_BANK, O_BANK = 4, 5, 6, 7
        SIDE = 256
        K_PLACES = [(g, 0) for g in range(QT)] + [(O_BANK, SIDE)]
        V_PLACES = [(OUT_BANK, 0)] * KD

        def projected(places, g):
            bank, col = places[g]
            return ps[:, bank, col:col + BATCH * TOKENS].rearrange("p (b n) -> p b n", b=BATCH)

        stage_loaded = [sem(f"stage_loaded{k}") for k in range(KD)]
        stage_hi = sem("stage_hi")
        stage_lo = sem("stage_lo")
        small_loaded = sem("small_loaded")
        ctx_loaded = sem("ctx_loaded")
        raw_loaded = {n: [sem(f"{n}_loaded{h}") for h in range(2)] for n in ("wk", "wki", "wv", "wvi")}
        zeroed = sem("zeroed")
        part_made = sem("part_made")
        part_copied = sem("part_copied")
        mask_step = sem("mask_step")
        kt_made = sem("kt_made")
        k_hi_done = sem("k_hi_done")
        k_lo_done = sem("k_lo_done")
        vt_made = sem("vt_made")
        vt_copied = sem("vt_copied")
        v_made = sem("v_made")
        v_copied = sem("v_copied")
        q_made = sem("q_made")
        q_hi_done = sem("q_hi_done")
        q_lo_done = sem("q_lo_done")
        scores_made = sem("scores_made")
        scores_used = sem("scores_used")
        text_max_done = sem("text_max_done")
        img_max_done = sem("img_max_done")
        shifted = sem("shifted")
        exp_done = sem("exp_done")
        sums_done = sem("sums_done")
        rden_done = sem("rden_done")
        prob_done = sem("prob_done")
        t_made = sem("t_made")
        t_copied = sem("t_copied")
        o_made = sem("o_made")
        o_hi_done = sem("o_hi_done")
        o_lo_done = sem("o_lo_done")
        out_made = sem("out_made")
        res_loaded = [sem(f"res_loaded{k}") for k in range(2)]
        late_loaded = [sem(f"late_loaded{k}") for k in range(LATE)]
        finished = sem("finished")
        stored = [sem(f"stored{k}") for k in range(2)]

        def num(i, c, each=1, plus=0):
            return i * (each * PER_TURN) + (each * c + plus)

        def place(i, c):
            return (c // KD) % BATCH, i + c // PER_TURN, c % KD

        def turns(eng, prologue, step, epilogue):
            prologue()
            for c in range(KD):
                step(0, c)
            with eng.Fori(0, (UNITS - PER_TURN) // PER_TURN) as i:
                for c in range(KD, KD + PER_TURN):
                    step(i, c)
            for c in range(UNITS - KD, UNITS):
                step(0, c)
            epilogue()

        def exists(i, c):
            return not isinstance(i, int) or 0 <= c < UNITS

        def is_early(i, c):
            return isinstance(i, int) and c < KD

        def is_late(i, c):
            return isinstance(i, int) and c >= UNITS - LATE

        def out_tile(i, c):
            if is_late(i, c):
                k = c - (UNITS - LATE)
                return stage[:, k, 0:W], late_loaded[k], 16
            return res[:, c % 2, :], res_loaded[c % 2], i * (16 * PER_TURN // 2) + 16 * (c // 2 + 1)

        G_WQ, G_X0, G_X1, G_WO = range(4)

        def x_group(c):
            return c // KD + 2 if c // KD >= 2 else G_X0 + c // KD

        def stage_jobs(i, c):
            at = c % KD
            if at < 2:
                return [("x", c - at + KD + k) for k in ((0, 1, 2), (3, 4))[at] if exists(i, c - at + KD)]
            if isinstance(i, int) and c in (2, 3):
                return [("w_out", k) for k in ((0, 1, 2), (3, 4))[c - 2]]
            return []

        def load_raw(eng, name, pair, src, halves=(0, 1)):
            for h in halves:
                eng.dma_start(pair[h][:, :, :],
                              src[4 * h:4 * h + 4].rearrange("k p n -> p k n")).then_inc(raw_loaded[name][h], 16)

        block = es.enter_context(nc.Block())

        @block.sync
        def _(sp):
            def load(group, kt, dst_w, src, turn=0):
                job = group * KD + kt
                if group >= 1:
                    sp.wait_ge(stage_lo, turn + job - KD + 1)
                sp.dma_start(stage[:, kt, 0:dst_w], src).then_inc(stage_loaded[kt], 16)

            def residual(i, c):
                tile, loaded, _ = out_tile(i, c)
                if isinstance(i, int) and c < 2:
                    sp.wait_ge(v_made, KD)
                if (not isinstance(i, int) or c >= 2) and not is_late(i, c):
                    sp.wait_ge(stored[c % 2], i * (16 * PER_TURN // 2) + 16 * (c // 2))
                sp.dma_start(tile, x[num(i, c)]).then_inc(loaded, 16)

            def store(i, c):
                sp.wait_ge(finished, num(i, c, 1, 1))
                sp.dma_start(out[num(i, c)], out_tile(i, c)[0]).then_inc(stored[c % 2], 16)

            def prologue():
                sp.dma_start(ctx_sb[:, :, :], ctx).then_inc(ctx_loaded, 16)
                load_raw(sp, "wk", wk_raw, w_k, halves=(0,))
                for kt in range(KD):
                    load(G_WQ, kt, D, w_q[kt])
                sp.dma_start(box[:, :, :, :], bbox).then_inc(small_loaded, 16)
                sp.dma_start(grid_sb[:, :], grid).then_inc(small_loaded, 16)
                sp.dma_start(bias[:, :], b_out).then_inc(small_loaded, 16)
                sp.dma_start(eye_sb[:, :], eye).then_inc(small_loaded, 16)
                load_raw(sp, "wk", wk_raw, w_k, halves=(1,))
                for kt in range(KD):
                    load(G_X0, kt, W, x[kt])
                load_raw(sp, "wki", wki_raw, w_k_ip)
                load_raw(sp, "wv", wv_raw, w_v)
                load_raw(sp, "wvi", wvi_raw, w_v_ip)

            def step(i, c):
                for what, k in stage_jobs(i, c):
                    if what == "x":
                        load(x_group(k), k % KD, W, x[num(i, k)], turn=i * PER_TURN)
                    else:
                        load(G_WO, k, D, w_out[k])
                if exists(i, c - BEHIND_OUT + 1):
                    residual(i, c - BEHIND_OUT + 1)
                if exists(i, c - BEHIND_OUT):
                    store(i, c - BEHIND_OUT)

            def epilogue():
                for c in range(UNITS - KD + 1, UNITS):
                    residual(0, c)
                for c in range(UNITS - KD, UNITS):
                    store(0, c)
                for k in range(2):
                    sp.wait_ge(stored[k], 16 * (UNITS // 2))

            turns(sp, prologue, step, epilogue)

        @block.gpsimd
        def _(pool):
            def low(group, kt, turn, width, raw_chunk, hi, lo):
                job = group * KD + kt
                pool.wait_ge(stage_hi, turn + job + 1)
                nc.gpsimd.tensor_tensor(lo, raw_chunk, hi.bitcast(F32), ALU.subtract).then_inc(stage_lo, 1)

            def x_low(i, c):
                b, _, kt = place(i, c)
                low(x_group(c), kt, i * PER_TURN, W, stage[:, kt, 0:W], x_hi[:, b, kt, :], x_lo[:, b, kt, :])

            def prologue():
                for kt in range(KD):
                    low(G_WQ, kt, 0, D, stage[:, kt, :], wq_hi[:, kt, :], wq_lo[:, kt, :])

            def step(i, c):
                par = c % 2
                pool.wait_ge(rden_done, num(i, c, 1, 1))
                e = prob[:, par, :, :].rearrange("p q (h k) -> p (q h) k", k=TOKENS)
                nc.gpsimd.tensor_tensor(e[:, :, 0:TEXT], e[:, :, 0:TEXT],
                                        rden[:, par, 0, :].unsqueeze(2).to_broadcast([P, QT * HG, TEXT]), ALU.mult)
                nc.gpsimd.tensor_tensor(e[:, :, TEXT:TOKENS], e[:, :, TEXT:TOKENS],
                                        rden[:, par, 1, :].unsqueeze(2).to_broadcast([P, QT * HG, IMG]),
                                        ALU.mult).then_inc(prob_done, 1)
                for what, k in stage_jobs(i, c - 1) if exists(i, c - 1) else []:
                    if what == "x":
                        x_low(i, k)
                    else:
                        low(G_WO, k, 0, D, stage[:, k, :], wo_hi[:, k, :], wo_lo[:, k, :])

            turns(pool, prologue, step, lambda: None)

        @block.scalar
        def _(act):
            def high(group, kt, turn, i16, raw_chunk, hi):
                act.wait_ge(stage_loaded[kt], i16 + 16 * (group + 1))
                nc.scalar.activation(hi, raw_chunk, ACT.Copy).then_inc(stage_hi, 1)

            def x_high(i, c):
                b, _, kt = place(i, c)
                if not isinstance(i, int) or c >= 2 * KD:
                    act.wait_ge(q_made, num(i, (c // KD - 1) * KD))
                high(x_group(c), kt, i * PER_TURN, i * (16 * BATCH), stage[:, kt, 0:W], x_hi[:, b, kt, :])

            def q_high(i, c):
                act.wait_ge(q_made, num(i, c, 1, 1))
                if not isinstance(i, int) or c >= 2:
                    act.wait_ge(scores_made, num(i, c - 2, 2, 2))
                nc.scalar.activation(q_hi[:, c % 2, :], ps[:, Q_BANK, :], ACT.Copy, scale=SCALE).then_inc(q_hi_done, 1)

            def exp(i, c):
                act.wait_ge(shifted, num(i, c, 1, 1))
                nc.scalar.activation(prob[:, c % 2, :, :], prob[:, c % 2, :, :], ACT.Exp).then_inc(exp_done, 1)

            def prologue():
                for kt in range(KD):
                    high(G_WQ, kt, 0, 0, stage[:, kt, :], wq_hi[:, kt, :])
                for kt in range(KD):
                    x_high(0, kt)
                q_high(0, 0)
                copy_part(0)
                act.wait_ge(zeroed, 1)
                for g in range(KD):
                    act.wait_ge(kt_made, g + 1)
                    for j in range(HG):
                        rows = slice(DH * j, DH * j + DH)
                        last = nc.scalar.activation(k_hi[rows, :, g, TOKENS * j:TOKENS * j + TOKENS],
                                                    projected(K_PLACES, g)[rows], ACT.Copy)
                    last.then_inc(k_hi_done, 1)
                q_high(0, 1)
                exp(0, 0)

            def copy_vt(g):
                act.wait_ge(vt_made, g + 1)
                nc.scalar.activation(vt[:, :, :], projected(V_PLACES, g), ACT.Copy).then_inc(vt_copied, 1)

            def copy_v(g):
                act.wait_ge(v_made, g + 1)
                nc.scalar.activation(v[0:TOKENS, :, P * g:P * g + P],
                                     ps[0:TOKENS, OUT_BANK, SIDE:SIDE + BATCH * P].rearrange("p (b n) -> p b n", b=BATCH),
                                     ACT.Copy).then_inc(v_copied, 1)

            def copy_part(n):
                act.wait_ge(part_made, n + 1)
                nc.scalar.activation(img_part[:, 0:512], ps[:, T_BANK, :], ACT.Copy)
                nc.scalar.activation(img_part[:, 512:D], ps[:, O_BANK, 0:D - 512], ACT.Copy).then_inc(part_copied, 1)

            def step(i, c):
                b, t, g = place(i, c)
                if isinstance(i, int) and c == 0:
                    copy_part(1)
                if is_early(i, c):
                    copy_vt(c)
                if exists(i, c + AHEAD_Q) and not is_early(i, c):
                    q_high(i, c + AHEAD_Q)
                for j in range(HG):
                    act.wait_ge(t_made, num(i, c, HG, j + 1))
                    if j == 0 and (not isinstance(i, int) or c >= 1):
                        act.wait_ge(o_made, num(i, c))
                    nc.scalar.activation(prob_t[0:TOKENS, j, :], ps[0:TOKENS, T_BANK + j % 2, :], ACT.Copy).then_inc(t_copied, 1)
                    if j == 1 and is_early(i, c):
                        copy_v(c)
                    if j == is_early(i, c) and exists(i, c + AHEAD_S):
                        exp(i, c + AHEAD_S)
                    if j == 2 and is_early(i, c):
                        q_high(i, c + AHEAD_Q)
                act.wait_ge(o_made, num(i, c, 1, 1))
                if not isinstance(i, int) or c >= 2 * KD:
                    act.wait_ge(out_made, num(i, (c // KD - 1) * KD))
                nc.scalar.activation(o_hi[:, b, g, :], ps[:, O_BANK, :], ACT.Copy).then_inc(o_hi_done, 1)
                for what, k in stage_jobs(i, c):
                    if what == "x":
                        x_high(i, k)
                    else:
                        high(G_WO, k, 0, 0, stage[:, k, :], wo_hi[:, k, :])

            turns(act, prologue, step, lambda: None)

        @block.vector
        def _(dve):
            def q_low(i, c):
                dve.wait_ge(q_hi_done, num(i, c, 1, 1))
                nc.vector.scalar_tensor_tensor(out=q_lo[:, c % 2, :], in0=ps[:, Q_BANK, :], scalar=SCALE,
                                               in1=q_hi[:, c % 2, :].bitcast(F32), op0=ALU.mult,
                                               op1=ALU.subtract).then_inc(q_lo_done, 1)

            def shift_pair(i, c, p):
                b, t, g = place(i, c)
                par, qs = c % 2, slice(2 * p, 2 * p + 2)
                s = ps[:, qs, 0:GW].rearrange("p q (h k) -> p q h k", k=TOKENS)
                e = prob[:, par, qs, :].rearrange("p q (h k) -> p q h k", k=TOKENS)
                dve.wait_ge(scores_made, num(i, c, 2, p + 1))
                nc.vector.tensor_reduce(text_max[:, par, qs, :], s[:, :, :, 0:TEXT], AX_X, ALU.max).then_inc(text_max_done, 1)
                if p == 0 and (not isinstance(i, int) or c >= 2):
                    dve.wait_ge(t_made, num(i, c - 2, HG, HG))
                nc.vector.tensor_tensor(e[:, :, :, TEXT:TOKENS], s[:, :, :, TEXT:TOKENS],
                                        mask[:, b, t, qs, :].unsqueeze(2).to_broadcast([P, 2, HG, IMG]), ALU.add)
                dve.wait_ge(text_max_done, num(i, c, 2, p + 1))
                nc.vector.tensor_tensor(e[:, :, :, 0:TEXT], s[:, :, :, 0:TEXT],
                                        text_max[:, par, qs, :].unsqueeze(3).to_broadcast([P, 2, HG, TEXT]),
                                        ALU.subtract).then_inc(scores_used, 1)

            def shift_img(i, c):
                par = c % 2
                e = prob[:, par, :, :].rearrange("p q (h k) -> p (q h) k", k=TOKENS)[:, :, TEXT:TOKENS]
                m = img_max[:, par, :, :].rearrange("p q h -> p (q h)")
                dve.wait_ge(scores_used, num(i, c, 2, 2))
                nc.vector.tensor_reduce(m, e, AX_X, ALU.max).then_inc(img_max_done, 1)
                dve.wait_ge(img_max_done, num(i, c, 1, 1))
                nc.vector.tensor_tensor(e, e, m.unsqueeze(2).to_broadcast([P, QT * HG, IMG]),
                                        ALU.subtract).then_inc(shifted, 1)

            def sums(i, c):
                par = c % 2
                e = prob[:, par, :, :].rearrange("p q (h k) -> p (q h) k", k=TOKENS)
                dve.wait_ge(exp_done, num(i, c, 1, 1))
                nc.vector.tensor_reduce(den[:, par, 0, :], e[:, :, 0:TEXT], AX_X, ALU.add)
                nc.vector.tensor_reduce(den[:, par, 1, :], e[:, :, TEXT:TOKENS], AX_X, ALU.add).then_inc(sums_done, 1)
                dve.wait_ge(sums_done, num(i, c, 1, 1))
                if not isinstance(i, int) or c >= 2:
                    dve.wait_ge(prob_done, num(i, c - 2, 1, 1))
                nc.vector.reciprocal(rden[:, par, :, :], den[:, par, :, :]).then_inc(rden_done, 1)

            def finish(i, c, bank=OUT_BANK):
                tile, loaded, n = out_tile(i, c)
                dve.wait_ge(out_made, num(i, c, 1, 1))
                dve.wait_ge(loaded, n)
                nc.vector.scalar_tensor_tensor(out=tile, in0=ps[:, bank, :],
                                               scalar=bias[:, c % KD:c % KD + 1], in1=tile,
                                               op0=ALU.add, op1=ALU.add).then_inc(finished, 1)

            def masks():
                steps = [0]

                def then(ins):
                    steps[0] += 1
                    ins.then_inc(mask_step, 1)
                    dve.wait_ge(mask_step, steps[0])

                blocks = [P, TILES * QT, BOXES]
                gx = grid_sb[:, 0:1].unsqueeze(2).to_broadcast(blocks)
                gy = grid_sb[:, 1:].unsqueeze(2).to_broadcast(blocks)
                inside = prob[:, 0, 0, 0:BATCH * TILES * QT * BOXES].rearrange("p (b t m) -> p b t m", b=BATCH, m=BOXES)
                test = prob[:, 0, 1, 0:BATCH * TILES * QT * BOXES].rearrange("p (b t m) -> p b t m", b=BATCH, m=BOXES)
                any_in = prob[:, 0, 2, 0:BATCH * TILES * QT].rearrange("p (b t) -> p b t", b=BATCH)
                dve.wait_ge(small_loaded, 64)
                for b in range(BATCH):
                    edge = [box[:, b, :, k].unsqueeze(1).to_broadcast(blocks) for k in range(4)]
                    then(nc.vector.tensor_tensor(inside[:, b], gx, edge[0], ALU.is_ge))
                    for coord, side, op in ((gx, 2, ALU.is_le), (gy, 1, ALU.is_ge), (gy, 3, ALU.is_le)):
                        then(nc.vector.tensor_tensor(test[:, b], coord, edge[side], op))
                        then(nc.vector.tensor_tensor(inside[:, b], inside[:, b], test[:, b], ALU.mult))
                    m = mask[:, b, :, :, :].rearrange("p t q k -> p (t q) k")
                    then(nc.vector.tensor_scalar(m[:, :, DUMMY:IMG], inside[:, b], -NEG, NEG, ALU.mult, ALU.add))
                    then(nc.vector.tensor_reduce(any_in[:, b], inside[:, b], AX_X, ALU.max))
                    then(nc.vector.tensor_scalar(m[:, :, 0:DUMMY],
                                                 any_in[:, b].unsqueeze(2).to_broadcast([P, TILES * QT, DUMMY]),
                                                 NEG, None, ALU.mult))

            def prologue():
                nc.vector.memset(k_hi[:, :, :, :].bitcast(F32), 0.0)
                nc.vector.memset(k_lo[:, :, :, :].bitcast(F32), 0.0)
                nc.vector.memset(prob_t[64:P, :, :], 0.0)
                nc.vector.memset(v[:, :, :], 0.0).then_inc(zeroed, 1)
                masks()
                dve.wait_ge(stage_lo, KD)
                for kt in range(KD):
                    dve.wait_ge(stage_hi, KD + kt + 1)
                    nc.vector.tensor_tensor(x_lo[:, 0, kt, :], stage[:, kt, 0:W], x_hi[:, 0, kt, :].bitcast(F32),
                                            ALU.subtract).then_inc(stage_lo, 1)
                q_low(0, 0)
                dve.wait_ge(zeroed, 1)
                for g in range(KD):
                    dve.wait_ge(k_hi_done, g + 1)
                    for j in range(HG):
                        rows = slice(DH * j, DH * j + DH)
                        cols = slice(TOKENS * j, TOKENS * j + TOKENS)
                        last = nc.vector.tensor_tensor(
                            k_lo[rows, :, g, cols], projected(K_PLACES, g)[rows],
                            k_hi[rows, :, g, cols].bitcast(F32), ALU.subtract)
                    last.then_inc(k_lo_done, 1)
                q_low(0, 1)
                shift_pair(0, 0, 0)
                shift_pair(0, 0, 1)
                shift_img(0, 0)
                sums(0, 0)

            def step(i, c):
                if exists(i, c + AHEAD_S):
                    shift_pair(i, c + AHEAD_S, 0)
                if exists(i, c - 1):
                    o_low(i, c - 1)
                if exists(i, c + AHEAD_S):
                    shift_pair(i, c + AHEAD_S, 1)
                    shift_img(i, c + AHEAD_S)
                if exists(i, c + AHEAD_Q):
                    q_low(i, c + AHEAD_Q)
                if exists(i, c + AHEAD_S):
                    sums(i, c + AHEAD_S)
                if exists(i, c - BEHIND_OUT):
                    finish(i, c - BEHIND_OUT)

            def o_low(i, c):
                b, t, g = place(i, c)
                dve.wait_ge(o_hi_done, num(i, c, 1, 1))
                nc.vector.tensor_tensor(o_lo[:, b, g, :], ps[:, O_BANK, :], o_hi[:, b, g, :].bitcast(F32),
                                        ALU.subtract).then_inc(o_lo_done, 1)

            def epilogue():
                o_low(0, UNITS - 1)
                for c in range(UNITS - KD, UNITS):
                    finish(0, c, c - (UNITS - KD))

            turns(dve, prologue, step, epilogue)

        @block.tensor
        def _(pe):
            whole = range(3 * KD)

            def three_pass(bank, w_hi, w_lo, m_hi, m_lo, b, g, part):
                cols = slice(P * g, P * g + P)
                steps = [s for kt in range(KD) for s in ((w_hi, m_hi, kt), (w_hi, m_lo, kt), (w_lo, m_hi, kt))]
                for n in part:
                    w, m, kt = steps[n]
                    last = nc.tensor.matmul(ps[:, bank, :], w[:, kt, cols], m[:, b, kt, :],
                                            start=(n == 0), stop=(n == len(steps) - 1))
                return last

            def make_q(i, c, part):
                b, t, g = place(i, c)
                if part[0] == 0:
                    if not isinstance(i, int) or c >= 1:
                        pe.wait_ge(q_lo_done, num(i, c))
                    if g == 0:
                        pe.wait_ge(stage_lo, (i * PER_TURN) + (x_group(c) + 1) * KD)
                last = three_pass(Q_BANK, wq_hi, wq_lo, x_hi, x_lo, b, g, part)
                if part[-1] == 3 * KD - 1:
                    last.then_inc(q_made, 1)

            def make_scores(i, c, p):
                b, t, g = place(i, c)
                if p == 0:
                    pe.wait_ge(q_lo_done, num(i, c, 1, 1))
                if not isinstance(i, int) or c >= 1:
                    pe.wait_ge(scores_used, num(i, c - 1, 2, p + 1))
                for q in (2 * p, 2 * p + 1):
                    blk = slice(P * q, P * q + P)
                    o = ps[:, q, 0:GW]
                    nc.tensor.matmul(o, q_hi[:, c % 2, blk], k_hi[:, b, g, :], start=True, stop=False)
                    nc.tensor.matmul(o, q_hi[:, c % 2, blk], k_lo[:, b, g, :], start=False, stop=False)
                    last = nc.tensor.matmul(o, q_lo[:, c % 2, blk], k_hi[:, b, g, :], start=False, stop=True)
                last.then_inc(scores_made, 1)

            def transpose(i, c, j):
                if j == 0:
                    pe.wait_ge(prob_done, num(i, c, 1, 1))
                    if not isinstance(i, int) or c >= 1:
                        pe.wait_ge(t_copied, num(i, c - 1, HG, HG - 1))
                elif j == 1:
                    if not isinstance(i, int) or c >= 1:
                        pe.wait_ge(o_lo_done, num(i, c))
                else:
                    pe.wait_ge(t_copied, num(i, c, HG, j - 1))
                for q in range(QT):
                    last = nc.tensor.transpose(ps[0:TOKENS, T_BANK + j % 2, P * q:P * q + P],
                                               prob[:, c % 2, q, TOKENS * j:TOKENS * j + TOKENS], ident)
                last.then_inc(t_made, 1)

            def make_o(i, c):
                b, t, g = place(i, c)
                pe.wait_ge(t_copied, num(i, c, HG, HG))
                for j in range(HG):
                    last = nc.tensor.matmul(ps[DH * j:DH * j + DH, O_BANK, :],
                                            v[:, b, P * g + DH * j:P * g + DH * j + DH], prob_t[:, j, :],
                                            start=True, stop=True)
                last.then_inc(o_made, 1)

            def make_out(i, c, part):
                b, t, g = place(i, c)
                if part[0] == 0:
                    if g == 0:
                        pe.wait_ge(o_lo_done, num(i, c, 1, KD))
                        if c // KD % BATCH == 0:
                            pe.wait_ge(stage_lo, (G_WO + 1) * KD)
                    if not isinstance(i, int) or c >= 1:
                        pe.wait_ge(finished, num(i, c))
                last = three_pass(OUT_BANK, wo_hi, wo_lo, o_hi, o_lo, b, g, part)
                if part[-1] == 3 * KD - 1:
                    last.then_inc(out_made, 1)

            def make_last(kt):
                pe.wait_ge(o_lo_done, UNITS - KD + kt + 1)
                for g in range(KD):
                    last = three_pass(g, wo_hi, wo_lo, o_hi, o_lo, BATCH - 1, g, whole[3 * kt:3 * kt + 3])
                    if kt == KD - 1:
                        last.then_inc(out_made, 1)

            def image_part(n, name, raw):
                for kt in range(KC):
                    if kt % 4 == 0:
                        pe.wait_ge(raw_loaded[name][kt // 4], 16)
                    rows = slice(IMG_PAD * (kt % 4), IMG_PAD * (kt % 4) + IMG_PAD)
                    for bank, cols in ((T_BANK, slice(0, 512)), (O_BANK, slice(512, D))):
                        last = nc.tensor.matmul(ps[rows, bank, 0:cols.stop - cols.start],
                                                ctx_sb[:, kt, BATCH * TEXT:CTX_COLS], raw[kt // 4][:, kt % 4, cols],
                                                start=(kt < 4), stop=(kt >= 4))
                last.then_inc(part_made, 1)

            def project_text(places, name, raw, g, half):
                pe.wait_ge(raw_loaded[name][half], 16)
                for kt in range(KC // 2 * half, KC // 2 * (half + 1)):
                    text = ctx_sb[:, kt, 0:BATCH * TEXT].rearrange("p (b n) -> p b n", b=BATCH)
                    nc.tensor.matmul(projected(places, g)[:, :, 0:TEXT], raw[half][:, kt % 4, P * g:P * g + P],
                                     text, start=(kt == 0), stop=(kt == KC - 1))

            def fold_image(places, g, made):
                nc.tensor.matmul(projected(places, g)[:, :, TEXT:TOKENS], img_part[:, P * g:P * g + P],
                                 fold.rearrange("p (b n) -> p b n", b=BATCH), start=True, stop=True).then_inc(made, 1)

            def prologue():
                pe.wait_ge(ctx_loaded, 16)
                for half in range(2):
                    for g in range(KD):
                        project_text(K_PLACES, "wk", wk_raw, g, half)
                make_q(0, 0, whole)
                image_part(0, "wki", wki_raw)
                make_q(0, 1, whole[0:5])
                pe.wait_ge(part_copied, 1)
                pe.wait_ge(small_loaded, 64)
                for g in range(KD):
                    fold_image(K_PLACES, g, kt_made)
                make_q(0, 1, whole[5:15])
                for half in range(2):
                    project_text(V_PLACES, "wv", wv_raw, 0, half)
                pe.wait_ge(k_lo_done, KD)
                make_scores(0, 0, 0)
                make_scores(0, 0, 1)

            def transpose_v(g):
                pe.wait_ge(vt_copied, g + 1)
                for b in range(BATCH):
                    last = nc.tensor.transpose(ps[0:TOKENS, OUT_BANK, SIDE + P * b:SIDE + P * b + P], vt[:, b, :], ident)
                last.then_inc(v_made, 1)

            def early_step(c):
                make_scores(0, c + AHEAD_S, 0)
                if c > 0:
                    project_text(V_PLACES, "wv", wv_raw, c, 1)
                make_q(0, c + AHEAD_Q, whole[0:5])
                if c > 0:
                    fold_image(V_PLACES, c, vt_made)
                make_scores(0, c + AHEAD_S, 1)
                make_q(0, c + AHEAD_Q, whole[5:8])
                if c == 0:
                    image_part(1, "wvi", wvi_raw)
                    make_q(0, c + AHEAD_Q, whole[8:12])
                    pe.wait_ge(part_copied, 2)
                    fold_image(V_PLACES, c, vt_made)
                transpose(0, c, 0)
                transpose(0, c, 1)
                transpose_v(c)
                if c > 0:
                    make_q(0, c + AHEAD_Q, whole[8:12])
                transpose(0, c, 2)
                make_q(0, c + AHEAD_Q, whole[12:15])
                transpose(0, c, 3)
                pe.wait_ge(v_copied, c + 1)
                if c + 1 < KD:
                    project_text(V_PLACES, "wv", wv_raw, c + 1, 0)
                make_o(0, c)

            def step(i, c):
                if is_early(i, c):
                    early_step(c)
                    return
                if exists(i, c + AHEAD_S):
                    make_scores(i, c + AHEAD_S, 0)
                if exists(i, c + AHEAD_Q):
                    make_q(i, c + AHEAD_Q, whole[0:8])
                if exists(i, c + AHEAD_S):
                    make_scores(i, c + AHEAD_S, 1)
                if exists(i, c + AHEAD_Q):
                    make_q(i, c + AHEAD_Q, whole[8:15])
                if isinstance(i, int) and c == UNITS - 1:
                    pe.wait_ge(scores_used, 2 * UNITS)
                    pe.wait_ge(q_lo_done, UNITS)
                    make_last(0)
                    make_last(1)
                for j in range(HG):
                    transpose(i, c, j)
                    if exists(i, c - BEHIND_OUT):
                        make_out(i, c - BEHIND_OUT, whole[max(4 * j - 1, 0):4 * j + 3])
                make_o(i, c)

            def epilogue():
                for kt in range(2, KD):
                    make_last(kt)

            turns(pe, prologue, step, epilogue)


def kernel(x, ctx_2048, fside_Bx4x4_0, L0_xattn_w_q, L0_xattn_w_k, L0_xattn_w_v, L0_xattn_w_k_ip,
           L0_xattn_w_v_ip, L0_xattn_w_out, L0_xattn_b_out):
    import numpy as np
    import concourse.bacc as bacc
    from concourse.bass_utils import run_bass_kernel_spmd

    xs = np.arange(GRID_W, dtype=np.float32) / np.float32(GRID_W - 1)
    ys = np.arange(GRID_H, dtype=np.float32) / np.float32(GRID_H - 1)
    p = np.arange(P)
    blocks = np.arange(TILES * QT)
    grid = np.concatenate([xs[p % GRID_W][:, None], ys[2 * blocks[None, :] + p[:, None] // GRID_W]], axis=1)

    def chunks(w):
        return np.asarray(w).reshape(-1, P, D)

    tokens = np.asarray(ctx_2048).reshape(BATCH, TOKENS, KC, P).transpose(3, 2, 0, 1)
    text = tokens[:, :, :, 0:TEXT].reshape(P, KC, BATCH * TEXT)
    image = tokens[:, :, :, TEXT:].reshape(P, KC, BATCH * IMG)
    arrays = {
        "x": np.asarray(x).reshape(BATCH, TILES, W, KD, P).transpose(1, 0, 3, 4, 2).reshape(UNITS, P, W),
        "ctx": np.concatenate([text, image, np.zeros((P, KC, IMG_PAD - BATCH * IMG), np.float32)], axis=2),
        "bbox": np.broadcast_to(np.asarray(fside_Bx4x4_0)[None], (P, BATCH, BOXES, 4)),
        "grid": grid,
        "eye": np.concatenate([np.eye(P), (p % IMG_PAD)[:, None] == np.arange(BATCH * IMG)], axis=1).astype(np.float32),
        "w_q": chunks(L0_xattn_w_q), "w_k": chunks(L0_xattn_w_k), "w_v": chunks(L0_xattn_w_v),
        "w_k_ip": chunks(L0_xattn_w_k_ip), "w_v_ip": chunks(L0_xattn_w_v_ip), "w_out": chunks(L0_xattn_w_out),
        "b_out": np.asarray(L0_xattn_b_out).reshape(KD, P).T,
    }
    arrays = {k: np.ascontiguousarray(a) for k, a in arrays.items()}
    nc = bacc.Bacc("TRN2", target_bir_lowering=False, num_devices=1)
    args = {k: nc.dram_tensor(f"in_{k}", a.shape, F32, kind="ExternalInput").ap() for k, a in arrays.items()}
    out = nc.dram_tensor("out_tiles", (UNITS, P, W), F32, kind="ExternalOutput").ap()
    xattn_kernel(nc, **args, out=out)
    r = run_bass_kernel_spmd(nc, [{f"in_{k}": a for k, a in arrays.items()}], core_ids=[0])
    got = np.asarray(r.results[0]["out_tiles"])
    return np.ascontiguousarray(got.reshape(TILES, BATCH, KD, P, W).transpose(1, 0, 4, 2, 3).reshape(BATCH, SEQ, D))
```
